# Optimizing a Trainium2 kernel written in Bass

```python
import numpy as np
import jax
import jax.numpy as jnp

def _softmax(x, axis=-1):
    return jax.nn.softmax(x, axis=axis)

def _gelu(x):
    return jax.nn.gelu(x, approximate=True)

def _silu(x):
    return jax.nn.silu(x)

def _sigmoid(x):
    return jax.nn.sigmoid(x)

def _layernorm(x, axis=-1, eps=1e-05):
    m = jnp.mean(x, axis=axis, keepdims=True)
    v = jnp.var(x, axis=axis, keepdims=True)
    return (x - m) / jnp.sqrt(v + eps)

def _scatter_add(tgt, idx, src, axis=0):
    return tgt.at[idx].add(src)

def _segment_sum(src, seg, n):
    return jax.ops.segment_sum(src, seg, n)
kernel_name = 'mk_gnn_preln_d4_gnn_r8_73004a'

def setup_inputs(seed: int=0):
    np.random.seed(seed)
    _w = jnp.asarray

    def _rec_inputs():
        import jax
        import jax.numpy as jnp
        _gk = jax.random.key(seed)
        x = -8.776e-05 + 1 * jax.random.normal(jax.random.fold_in(_gk, 1), (5000, 128), jnp.float32)
        _s = jax.random.randint(jax.random.fold_in(_gk, 2), (40000,), 0, 5000, jnp.int32)
        _d = jax.random.randint(jax.random.fold_in(_gk, 3), (40000,), 0, 5000, jnp.int32)
        _loop = jnp.arange(5000, dtype=jnp.int32)
        src = jnp.concatenate([_s, _d, _loop])
        dst = jnp.concatenate([_d, _s, _loop])
        _o = jnp.argsort(dst, stable=True)
        src = src[_o]
        dst = dst[_o]
        return (x, src, dst)
    x, src, dst = _rec_inputs()

    def _L0_gnn_setup():
        import jax, jax.numpy as jnp
        import numpy as np
        N = 5000
        E = 80000
        F_IN = 128
        F_OUT = 128
        EPS = 1e-06
        key = jax.random.key(seed)
        k1, k2, k3, k4, k5 = jax.random.split(key, 5)
        x = jax.random.normal(k1, (N, F_IN), dtype=jnp.float32)
        row = jax.random.randint(k2, (E,), 0, N, dtype=jnp.int32)
        col = jax.random.randint(k3, (E,), 0, N, dtype=jnp.int32)
        W = jax.random.normal(k4, (F_OUT, F_IN), dtype=jnp.float32) * (1.0 / np.sqrt(F_IN))
        b = jax.random.normal(k5, (F_OUT,), dtype=jnp.float32) * 0.01
        return {'x': x, 'row': row, 'col': col, 'W': W, 'b': b}
    _L0_gnn_all = _L0_gnn_setup()
    _L0_gnn_in = {k: v for k, v in _L0_gnn_all.items() if k in ('W', 'b')}
    del _L0_gnn_all

    def _L1_gnn_setup():
        import jax, jax.numpy as jnp
        import numpy as np
        N_NODES = 6250
        N_EDGES = 100000
        D = 128
        key = jax.random.key(seed)
        ks = jax.random.split(key, 6)
        feat = jax.random.normal(ks[0], (N_NODES, D), dtype=jnp.float32)
        src = jax.random.randint(ks[1], (N_EDGES,), 0, N_NODES)
        dst = jax.random.randint(ks[2], (N_EDGES,), 0, N_NODES)
        W_edge = jax.random.normal(ks[3], (D, 2 * D), dtype=jnp.float32) * (1.0 / np.sqrt(2 * D))
        W_node = jax.random.normal(ks[4], (D, D), dtype=jnp.float32) * (1.0 / np.sqrt(D))
        b_node = jax.random.normal(ks[5], (D,), dtype=jnp.float32) * 0.01
        return {'feat': feat, 'src': src, 'dst': dst, 'W_edge': W_edge, 'W_node': W_node, 'b_node': b_node}
    _L1_gnn_all = _L1_gnn_setup()
    _L1_gnn_in = {k: v for k, v in _L1_gnn_all.items() if k in ('W_edge', 'W_node', 'b_node')}
    del _L1_gnn_all

    def _L2_gnn_setup():
        import jax, jax.numpy as jnp
        import numpy as np
        N_NODES = 6250
        HEADS = 16
        HEAD_DIM = 8
        IN_DIM = 128
        HID = HEADS * HEAD_DIM
        NEG_SLOPE = 0.2

        def _gat_conv(x, src, dst, W, a_src, a_dst, bias):
            N = x.shape[0]
            xh = (x @ W).reshape(N, HEADS, HEAD_DIM)
            al_s = jnp.einsum('nhc,hc->nh', xh, a_src)
            al_d = jnp.einsum('nhc,hc->nh', xh, a_dst)
            e = jax.nn.leaky_relu(al_s[src] + al_d[dst], NEG_SLOPE)
            m = jax.ops.segment_max(e, dst, num_segments=N)
            m = jnp.where(jnp.isfinite(m), m, 0.0)
            ex = jnp.exp(e - m[dst])
            denom = jax.ops.segment_sum(ex, dst, num_segments=N)
            alpha = ex / (denom[dst] + 1e-16)
            msg = xh[src] * alpha[:, :, None]
            out = jax.ops.segment_sum(msg, dst, num_segments=N)
            return out.reshape(N, HID) + bias
        key = jax.random.key(seed)
        ks = jax.random.split(key, 12)
        s = 1.0 / np.sqrt(IN_DIM)
        s2 = 1.0 / np.sqrt(HID)
        return {'x': jax.random.normal(ks[0], (N_NODES, IN_DIM), jnp.float32), 'edge_index': jax.random.randint(ks[1], (2, 100000), 0, N_NODES, jnp.int64), 'W1': jax.random.normal(ks[2], (IN_DIM, HID), jnp.float32) * s, 'a_src1': jax.random.normal(ks[3], (HEADS, HEAD_DIM), jnp.float32) * s, 'a_dst1': jax.random.normal(ks[4], (HEADS, HEAD_DIM), jnp.float32) * s, 'b1': jnp.zeros((HID,), jnp.float32), 'W2': jax.random.normal(ks[5], (HID, HID), jnp.float32) * s2, 'a_src2': jax.random.normal(ks[6], (HEADS, HEAD_DIM), jnp.float32) * s2, 'a_dst2': jax.random.normal(ks[7], (HEADS, HEAD_DIM), jnp.float32) * s2, 'b2': jnp.zeros((HID,), jnp.float32)}
    _L2_gnn_all = _L2_gnn_setup()
    _L2_gnn_in = {k: v for k, v in _L2_gnn_all.items() if k in ('W1', 'a_src1', 'a_dst1', 'b1', 'W2', 'a_src2', 'a_dst2', 'b2')}
    del _L2_gnn_all

    def _L3_gnn_setup():
        import jax, jax.numpy as jnp
        import numpy as np
        N = 6250
        E = 100000
        D_IN = 128
        HEADS = 2
        C = 64
        key = jax.random.key(seed)
        ks = jax.random.split(key, 10)
        scale = 1.0 / np.sqrt(D_IN)
        x = jax.random.normal(ks[0], (N, D_IN), dtype=jnp.float32)
        edge_index = jax.random.randint(ks[1], (2, E), 0, N, dtype=jnp.int64)
        Wq = jax.random.normal(ks[2], (D_IN, HEADS * C), dtype=jnp.float32) * scale
        Wk = jax.random.normal(ks[3], (D_IN, HEADS * C), dtype=jnp.float32) * scale
        Wv = jax.random.normal(ks[4], (D_IN, HEADS * C), dtype=jnp.float32) * scale
        Wskip = jax.random.normal(ks[5], (D_IN, HEADS * C), dtype=jnp.float32) * scale
        bq = jnp.zeros((HEADS * C,), dtype=jnp.float32)
        bk = jnp.zeros((HEADS * C,), dtype=jnp.float32)
        bv = jnp.zeros((HEADS * C,), dtype=jnp.float32)
        bskip = jnp.zeros((HEADS * C,), dtype=jnp.float32)
        return {'x': x, 'edge_index': edge_index, 'Wq': Wq, 'bq': bq, 'Wk': Wk, 'bk': bk, 'Wv': Wv, 'bv': bv, 'Wskip': Wskip, 'bskip': bskip}
    _L3_gnn_all = _L3_gnn_setup()
    _L3_gnn_in = {k: v for k, v in _L3_gnn_all.items() if k in ('Wq', 'bq', 'Wk', 'bk', 'Wv', 'bv', 'Wskip', 'bskip')}
    del _L3_gnn_all
    return {'x': x, 'src': src, 'dst': dst, 'L0_gnn_W': _L0_gnn_in['W'], 'L0_gnn_b': _L0_gnn_in['b'], 'L1_gnn_W_edge': _L1_gnn_in['W_edge'], 'L1_gnn_W_node': _L1_gnn_in['W_node'], 'L1_gnn_b_node': _L1_gnn_in['b_node'], 'L2_gnn_W1': _L2_gnn_in['W1'], 'L2_gnn_a_src1': _L2_gnn_in['a_src1'], 'L2_gnn_a_dst1': _L2_gnn_in['a_dst1'], 'L2_gnn_b1': _L2_gnn_in['b1'], 'L2_gnn_W2': _L2_gnn_in['W2'], 'L2_gnn_a_src2': _L2_gnn_in['a_src2'], 'L2_gnn_a_dst2': _L2_gnn_in['a_dst2'], 'L2_gnn_b2': _L2_gnn_in['b2'], 'L3_gnn_Wq': _L3_gnn_in['Wq'], 'L3_gnn_bq': _L3_gnn_in['bq'], 'L3_gnn_Wk': _L3_gnn_in['Wk'], 'L3_gnn_bk': _L3_gnn_in['bk'], 'L3_gnn_Wv': _L3_gnn_in['Wv'], 'L3_gnn_bv': _L3_gnn_in['bv'], 'L3_gnn_Wskip': _L3_gnn_in['Wskip'], 'L3_gnn_bskip': _L3_gnn_in['bskip']}

def reference(x, src, dst, L0_gnn_W, L0_gnn_b, L1_gnn_W_edge, L1_gnn_W_node, L1_gnn_b_node, L2_gnn_W1, L2_gnn_a_src1, L2_gnn_a_dst1, L2_gnn_b1, L2_gnn_W2, L2_gnn_a_src2, L2_gnn_a_dst2, L2_gnn_b2, L3_gnn_Wq, L3_gnn_bq, L3_gnn_Wk, L3_gnn_bk, L3_gnn_Wv, L3_gnn_bv, L3_gnn_Wskip, L3_gnn_bskip):
    import jax
    import jax.numpy as jnp

    def _L0_gnn_ref(x, row, col, W, b):
        import jax, jax.numpy as jnp
        import numpy as np
        N = 5000
        E = 80000
        F_IN = 128
        F_OUT = 128
        EPS = 1e-06
        neigh_sum = jax.ops.segment_sum(x[col], row, num_segments=N)
        deg = jax.ops.segment_sum(jnp.ones((row.shape[0],), x.dtype), row, num_segments=N)
        neighbor_mean = neigh_sum / (deg[:, None] + EPS)
        return neighbor_mean @ W.T + b

    def _L1_gnn_ref(feat, src, dst, W_edge, W_node, b_node):
        import jax, jax.numpy as jnp
        import numpy as np
        N_NODES = 6250
        N_EDGES = 100000
        D = 128
        N = feat.shape[0]
        eh = jnp.concatenate([feat[src], feat[dst]], axis=1) @ W_edge.T
        eh = jax.nn.relu(eh)
        s = jax.ops.segment_sum(eh, dst, num_segments=N)
        cnt = jax.ops.segment_sum(jnp.ones((dst.shape[0],), feat.dtype), dst, num_segments=N)[:, None]
        h = jnp.where(cnt > 0, s / jnp.maximum(cnt, 1.0), 0.0)
        return jax.nn.relu(h @ W_node.T + b_node)

    def _L2_gnn_ref(x, edge_index, W1, a_src1, a_dst1, b1, W2, a_src2, a_dst2, b2):
        import jax, jax.numpy as jnp
        import numpy as np
        N_NODES = 6250
        HEADS = 16
        HEAD_DIM = 8
        IN_DIM = 128
        HID = HEADS * HEAD_DIM
        NEG_SLOPE = 0.2

        def _gat_conv(x, src, dst, W, a_src, a_dst, bias):
            N = x.shape[0]
            xh = (x @ W).reshape(N, HEADS, HEAD_DIM)
            al_s = jnp.einsum('nhc,hc->nh', xh, a_src)
            al_d = jnp.einsum('nhc,hc->nh', xh, a_dst)
            e = jax.nn.leaky_relu(al_s[src] + al_d[dst], NEG_SLOPE)
            m = jax.ops.segment_max(e, dst, num_segments=N)
            m = jnp.where(jnp.isfinite(m), m, 0.0)
            ex = jnp.exp(e - m[dst])
            denom = jax.ops.segment_sum(ex, dst, num_segments=N)
            alpha = ex / (denom[dst] + 1e-16)
            msg = xh[src] * alpha[:, :, None]
            out = jax.ops.segment_sum(msg, dst, num_segments=N)
            return out.reshape(N, HID) + bias
        N = x.shape[0]
        loops = jnp.arange(N, dtype=edge_index.dtype)
        src = jnp.concatenate([edge_index[0], loops])
        dst = jnp.concatenate([edge_index[1], loops])
        h = jax.nn.elu(_gat_conv(x, src, dst, W1, a_src1, a_dst1, b1))
        h = _gat_conv(h, src, dst, W2, a_src2, a_dst2, b2)
        return h

    def _L3_gnn_ref(x, edge_index, Wq, bq, Wk, bk, Wv, bv, Wskip, bskip):
        import jax, jax.numpy as jnp
        import numpy as np
        N = 6250
        E = 100000
        D_IN = 128
        HEADS = 2
        C = 64
        n = x.shape[0]
        src, dst = (edge_index[0], edge_index[1])
        q = (x @ Wq + bq).reshape(n, HEADS, C)
        k = (x @ Wk + bk).reshape(n, HEADS, C)
        v = (x @ Wv + bv).reshape(n, HEADS, C)
        alpha = (q[dst] * k[src]).sum(-1) * (1.0 / np.sqrt(C)).astype(np.float32)
        m = jax.ops.segment_max(alpha, dst, num_segments=n)
        a = jnp.exp(alpha - m[dst])
        denom = jax.ops.segment_sum(a, dst, num_segments=n)
        agg = jax.ops.segment_sum(a[:, :, None] * v[src], dst, num_segments=n)
        agg = agg / jnp.maximum(denom, 1e-16)[:, :, None]
        out = agg.reshape(n, HEADS * C) + (x @ Wskip + bskip)
        return out
    edge_index = jnp.stack([src, dst])
    h = jnp.maximum(_layernorm(x, axis=-1), 0.0)
    x = x + _L0_gnn_ref(h, src, dst, L0_gnn_W, L0_gnn_b)
    h = jnp.maximum(_layernorm(x, axis=-1), 0.0)
    x = x + _L1_gnn_ref(h, src, dst, L1_gnn_W_edge, L1_gnn_W_node, L1_gnn_b_node)
    h = jnp.maximum(_layernorm(x, axis=-1), 0.0)
    x = x + _L2_gnn_ref(h, edge_index, L2_gnn_W1, L2_gnn_a_src1, L2_gnn_a_dst1, L2_gnn_b1, L2_gnn_W2, L2_gnn_a_src2, L2_gnn_a_dst2, L2_gnn_b2)
    h = jnp.maximum(_layernorm(x, axis=-1), 0.0)
    x = x + _L3_gnn_ref(h, edge_index, L3_gnn_Wq, L3_gnn_bq, L3_gnn_Wk, L3_gnn_bk, L3_gnn_Wv, L3_gnn_bv, L3_gnn_Wskip, L3_gnn_bskip)
    return x

_drawn_inputs = setup_inputs


def setup_inputs(seed=0):
    import zlib

    import numpy as np

    out = dict(_drawn_inputs(seed))
    spreads = {'L2_gnn_b1': (0.0, 0.1),
     'L2_gnn_b2': (0.0, 0.1),
     'L3_gnn_bq': (0.0, 0.8),
     'L3_gnn_bk': (0.0, 2.0),
     'L3_gnn_bv': (0.0, 0.1),
     'L3_gnn_bskip': (0.0, 0.1)}
    factors = {'L0_gnn_b': 5.805,
     'L1_gnn_b_node': 7.231,
     'L2_gnn_a_src1': 4.073,
     'L2_gnn_a_dst1': 32.59,
     'L2_gnn_a_src2': 45.053,
     'L2_gnn_a_dst2': 171.363}
    for name, (base, spread) in spreads.items():
        noise = np.random.default_rng([zlib.crc32(name.encode()), seed]).standard_normal(out[name].shape)
        drawn = base * np.exp(spread * noise) if base else spread * noise
        out[name] = jnp.asarray(drawn.astype(out[name].dtype))
    for name, factor in factors.items():
        out[name] = (out[name] * factor).astype(out[name].dtype)
    return out
```

```python
from contextlib import ExitStack

import concourse.bass as bass
from concourse import mybir

F32 = mybir.dt.float32
BF16 = mybir.dt.bfloat16
I32 = mybir.dt.int32
ALU = mybir.AluOpType
ACT = mybir.ActivationFunctionType
AX = mybir.AxisListType

P = 128
G = 8
RING = 4
BIG = 1.0e30
LN_EPS = 1e-5
MEAN_EPS = 1e-6
SOFTMAX_EPS = 1e-16


class Signal:

    def __init__(self, sem, per=1, by=1):
        self.sem, self.per, self.by, self.base = sem, per, by, 0

    def done(self, ins):
        ins.then_inc(self.sem, self.by)

    def value(self, rnd, k=None):
        k = self.per if k is None else k + 1
        return (rnd * self.per + k) * self.by + self.base

    def wait(self, eng, rnd, k=None):
        v = self.value(rnd, k)
        if not isinstance(v, int) or v > self.base:
            eng.wait_ge(self.sem, v)

    def close(self, rounds):
        self.base += rounds * self.per * self.by


def program(nc, x, src, dst, w0, b0, w_edge, w_node, b_node, w1, as1, ad1, b1, w2, as2, ad2, b2,
            wq, bq, wk, bk, wv, bv, wskip, bskip, out):
    N, D = x.shape
    E = src.shape[0]
    T = -(-E // P)
    NB = -(-N // P)
    NP = NB * P
    STEPS = T + NB - 1
    NG = -(-STEPS // G)
    SC = -(-(NG * G) // P)
    SP_ = SC * P
    FULL, REST = N // P, N % P
    NBAT = NB // G
    HEADS1, HEADS3 = as1.shape[0], 2
    assert D == P and NB % G == 0 and REST and NG * G == STEPS and NG % RING == 0

    first_drams = {h: nc.dram_tensor(f"first_dram{h}", [SP_ * h, P], F32, kind="Internal").ap()
                   for h in (as1.shape[0], 2)}
    dst_pad = nc.dram_tensor("dst_pad", [T * P], I32, kind="Internal").ap()
    src_pad = nc.dram_tensor("src_pad", [T * P], I32, kind="Internal").ap()
    block_dram = nc.dram_tensor("block_dram", [SP_], I32, kind="Internal").ap()
    tables = [nc.dram_tensor(f"table{i}", [NP, w], F32, kind="Internal").ap()
              for i, w in enumerate((D, D, D + HEADS1, D + HEADS1, 2 * D))]

    ctx = ExitStack()
    with ctx:
        def sb(name, shape, dt=F32):
            return ctx.enter_context(nc.sbuf_tensor(name, shape, dt))

        def sem(name):
            return ctx.enter_context(nc.semaphore(name))

        X = sb("X", [P, NB, D])
        acc = sb("acc", [P, NB, D + HEADS1])
        nodeQ = sb("nodeQ", [P, NB, D])
        nodeD = sb("nodeD", [P, NB, HEADS1])
        nodeS = sb("nodeS", [P, NB, HEADS1])
        nodeM = sb("nodeM", [P, NB, HEADS1])
        deg = sb("deg", [P, NB, 1])
        srcT = sb("srcT", [P, SP_], I32)
        slotT = sb("slotT", [P, SP_])
        lastT = sb("lastT", [P, SP_])
        blk = sb("blk", [1, SP_], I32)
        ident = sb("ident", [P, P])
        iota = sb("iota", [P, P])
        GT = sb("GT", [P, RING, G, 2 * D])
        consts = sb("consts", [P, 3, 1])
        wbuf = sb("wbuf", [P, 4, 3 * D + D])
        bias = sb("bias", [P, 9, D])
        O = sb("O", [P, 2, G, P])
        Ot = sb("Ot", [P, 2, G, P])
        V = sb("V", [P, 2, G, D + HEADS1])
        prod = sb("prod", [P, G, D])
        lg = sb("lg", [P, 2, G * HEADS1])
        lg2 = sb("lg2", [P, G * HEADS1])
        first = sb("first", [P, RING, P])
        seg = sb("seg", [P, 2, P])
        lastmax = sb("lastmax", [P, 2, G, HEADS1 + 1])
        tmax = sb("tmax", [P, 2, G, HEADS1])
        pen = sb("pen", [P, 2, G])
        diff = sb("diff", [P, 2, G, HEADS1])
        resc = sb("resc", [P, 2, G, HEADS1])
        below = sb("below", [P, 2, G * HEADS1])
        Y = sb("Y", [P, G, D])
        Y2 = sb("Y2", [P, G, D])
        YT = sb("YT", [P, G, P])
        R = sb("R", [P, G, 2 * D])
        st = sb("st", [P, 4, G * HEADS1])

        psT = ctx.enter_context(nc.psum_tensor("psT", [P, G, P], F32))
        psD = ctx.enter_context(nc.psum_tensor("psD", [P, G, P], F32))
        psS = ctx.enter_context(nc.psum_tensor("psS", [P, 512], F32))
        psA = ctx.enter_context(nc.psum_tensor("psA", [P, 3, 512], F32))

        def agg(j, w):
            return psA[:, j // 3, (j % 3) * 160:(j % 3) * 160 + w]

        apart_sem = sem("apart")

        def apart(eng):
            eng.sem_inc(apart_sem, 1)

        chain_sems = {kind: Signal(sem(f"chain_{kind}"), 0, 16 if kind.endswith("dma") else 1)
                      for kind in ("compute", "sync_dma", "pool_dma")}

        def chain(stages, rounds=1):
            kinds = [who if who.endswith("dma") else "compute" for who, _ in stages]
            places, count = [], dict.fromkeys(chain_sems, 0)
            for kind in kinds:
                places.append(count[kind])
                count[kind] += 1
            for kind, sg in chain_sems.items():
                sg.per = count[kind]
            with nc.Block() as block:
                def body(eng, key, i):
                    for n, (who, fn) in enumerate(stages):
                        if who.split("_")[0] != key:
                            continue
                        if n:
                            chain_sems[kinds[n - 1]].wait(eng, i, places[n - 1])
                        elif rounds > 1:
                            sg = chain_sems[kinds[-1]]
                            sg.wait(eng, i - 1)
                        if rounds > 1 and kinds[n] == "compute":
                            apart(eng)
                        sg = chain_sems[kinds[n]]
                        fn(eng, i).then_inc(sg.sem, sg.by)

                def run(key):
                    def _(eng):
                        if not any(who.split("_")[0] == key for who, _ in stages):
                            return
                        if rounds == 1:
                            body(eng, key, 0)
                        else:
                            with eng.Fori(0, rounds) as i:
                                body(eng, key, i)
                    return _

                block.sync(run("sync"))
                block.gpsimd(run("pool"))
                block.scalar(run("scalar"))
                block.vector(run("vector"))
                block.tensor(run("tensor"))
            for sg in chain_sems.values():
                sg.close(rounds)

        load_sem = sem("load")
        c_sem = sem("const")
        zrow = sb("zrow", [1, P], I32)
        padrow = sb("padrow", [1, P], I32)
        vrow_i = Ot[0:1, :, :, :].rearrange("p a g e -> p a (g e)").bitcast(I32)
        vrow = [Y[0:1, :, :].rearrange("p g e -> p (g e)"), Y2[0:1, :, :].rearrange("p g e -> p (g e)")]
        vsb = O[:, :, :, :].rearrange("p a g e -> p a (g e)")
        vall = psD[:, :, :].rearrange("p a b -> p (a b)")
        sidx_i = sb("sidx_i", [P, SC], I32)
        sidx = sb("sidx", [P, 4, SC])
        tb_i = sb("tb_i", [P, 2, SC], I32)
        iota_i = sb("iota_i", [P, P], I32)
        hmask = sb("hmask", [P, HEADS1])
        acol = sb("acol", [P, 4])
        adiag = sb("adiag", [P, 4, HEADS1])
        wraw = V[:, :, :, :].rearrange("p a g e -> p (a g e)")[:, 0:10 * D].rearrange("p (k f) -> p k f", f=D)
        flat = GT[:, :, :, :].rearrange("p r g w -> p (r g w)")
        rows = [flat[:, i * SP_:(i + 1) * SP_].rearrange("p (c e) -> p c e", c=SC) for i in range(6)]
        dst_r, src_r, dst_f, src_f, last_r, first_r = rows
        dst_r, src_r = dst_r.bitcast(I32), src_r.bitcast(I32)

        W0, WEA, WEB, WN, W1R, W2R, WQR, WKR, WVR, WSR = range(10)
        n_loads = 0
        with nc.Block() as block:
            @block.sync
            def _(eng):
                n = 0

                def load(to, of):
                    nonlocal n
                    eng.dma_start(to, of).then_inc(load_sem, 16)
                    n += 1

                load(X[:, 0:FULL, :], x[0:FULL * P, :].rearrange("(b p) f -> p b f", p=P))
                for slot, w in ((W0, w0), (WEA, w_edge[:, 0:D]), (WEB, w_edge[:, D:2 * D]),
                                (WN, w_node), (W1R, w1), (W2R, w2), (WQR, wq), (WKR, wk),
                                (WVR, wv), (WSR, wskip)):
                    load(wraw[:, slot, :], w)
                for k, b in enumerate((b0, b_node, b1, b2, bk, bv, bq, bskip)):
                    load(bias[:, k, :], b.rearrange("(a f) -> a f", a=1).to_broadcast([P, D]))
                for k, a in enumerate((as1, ad1, as2, ad2)):
                    load(acol[:, k:k + 1], a.rearrange("h (c o) -> (h c) o", o=1))
                load(dst_pad[0:E].rearrange("(a n) -> a n", a=8), dst.rearrange("(a n) -> a n", a=8))
                load(src_pad[0:E].rearrange("(a n) -> a n", a=8), src.rearrange("(a n) -> a n", a=8))
                eng.wait_ge(c_sem, 3)
                load(X[0:REST, FULL, :], x[FULL * P:N, :])
                if T * P > E:
                    load(dst_pad[E:T * P].rearrange("(a n) -> a n", a=1), padrow[0:1, 0:T * P - E])
                    load(src_pad[E:T * P].rearrange("(a n) -> a n", a=1), zrow[0:1, 0:T * P - E])
                eng.wait_ge(load_sem, 16 * n)
                nonlocal n_loads
                n_loads = n

            @block.gpsimd
            def _(eng):
                eng.memset(zrow[:, :], 0).then_inc(c_sem, 1)
                eng.memset(padrow[:, :], 2 * NP).then_inc(c_sem, 1)
                eng.memset(X[:, FULL, :], 0.0).then_inc(c_sem, 1)
                eng.memset(ident[:, :], 0.0).then_inc(c_sem, 1)
                eng.memset(hmask[:, :], 1.0).then_inc(c_sem, 1)
                for k, value in enumerate((0.0, 1.0, -BIG)):
                    eng.memset(consts[:, k, :], value).then_inc(c_sem, 1)
                eng.wait_ge(c_sem, 8)
                eng.affine_select(out=ident[:, :], in_=ident[:, :], compare_op=ALU.not_equal, fill=1.0,
                                  base=0, pattern=[[-1, P]], channel_multiplier=1).then_inc(c_sem, 1)
                eng.affine_select(out=hmask[:, :], in_=hmask[:, :], compare_op=ALU.is_ge, fill=0.0,
                                  base=0, pattern=[[-(D // HEADS1), HEADS1]],
                                  channel_multiplier=1).then_inc(c_sem, 1)
                eng.wait_ge(c_sem, 10)
                eng.affine_select(out=hmask[:, :], in_=hmask[:, :], compare_op=ALU.is_ge, fill=0.0,
                                  base=D // HEADS1 - 1, pattern=[[D // HEADS1, HEADS1]],
                                  channel_multiplier=-1).then_inc(c_sem, 1)
                eng.iota(iota_i[:, :], pattern=[[1, P]], base=0, channel_multiplier=0).then_inc(c_sem, 1)
                eng.iota(sidx_i[:, :], pattern=[[P, SC]], base=0, channel_multiplier=1).then_inc(c_sem, 1)
                eng.iota(vrow_i[:, 1, 0:T], pattern=[[1, T]], base=0, channel_multiplier=0)\
                   .then_inc(c_sem, 1)

            @block.vector
            def _(eng):
                eng.wait_ge(c_sem, 14)
                eng.tensor_copy(iota[:, :], iota_i[:, :]).then_inc(c_sem, 1)
                eng.tensor_copy(sidx[:, 0, :], sidx_i[:, :]).then_inc(c_sem, 1)
                eng.tensor_copy(vrow[1][:, 0:T], vrow_i[:, 1, 0:T]).then_inc(c_sem, 1)
                eng.wait_ge(load_sem, 16 * n_loads)
                for k in range(4):
                    eng.tensor_scalar(adiag[:, k, :], hmask[:, :], acol[:, k:k + 1], None, ALU.mult)\
                       .then_inc(c_sem, 1)

        shift = P.bit_length() - 1
        assert P == 1 << shift
        e_rows = dst_pad.rearrange("(t e) -> t e", e=P)
        s_rows = src_pad.rearrange("(t e) -> t e", e=P)
        st_ = []

        def add(who, fn):
            st_.append((who, fn))

        add("sync_dma", lambda e, i: e.dma_start(vrow_i[:, 0, 0:T], e_rows[:, 0:1].rearrange("t o -> o t"),
                                                   allow_slow_non_contiguous=True))
        add("vector", lambda e, i: e.tensor_scalar(vrow_i[:, 1, 0:T], vrow_i[:, 0, 0:T], shift, None,
                                                   ALU.logical_shift_right))
        add("vector", lambda e, i: e.tensor_copy(vrow[0][:, 0:T], vrow_i[:, 1, 0:T]))
        add("vector", lambda e, i: e.tensor_tensor(vrow[0][:, 0:T], vrow[0][:, 0:T], vrow[1][:, 0:T], ALU.add))

        def spread(e, i):
            ins = None
            for a in range(0, T, 512):
                z = min(T, a + 512)
                ins = e.matmul(vall[:, a:z], iota_one[0:1, :], vrow[0][:, a:z], start=True, stop=True)
            return ins
        iota_one = sb("iota_one", [1, P])
        add("vector", lambda e, i: e.tensor_scalar(iota_one[:, :], iota[0:1, :], 0.0, 1.0, ALU.mult, ALU.add))
        add("tensor", spread)
        add("vector", lambda e, i: e.tensor_copy(vsb[:, 0, 0:T], vall[:, 0:T]))

        def count(e, i):
            for c in range(SC):
                ins = e.tensor_scalar(vsb[:, 1, 0:T], vsb[:, 0, 0:T], sidx[:, 0, c:c + 1], None,
                                      ALU.is_le, ALU.add, accum_out=sidx[:, 1, c:c + 1])
                if c < SC - 1:
                    own.done(ins)
                    own.wait(e, c)
            return ins
        own = Signal(sem("own"))
        add("vector", count)
        add("vector", lambda e, i: e.tensor_scalar(sidx[:, 1, :], sidx[:, 1, :], -1.0, None, ALU.add))
        add("vector", lambda e, i: e.tensor_tensor(sidx[:, 2, :], sidx[:, 0, :], sidx[:, 1, :], ALU.subtract))
        add("vector", lambda e, i: e.tensor_scalar(sidx[:, 3, :], sidx[:, 2, :], float(P), None, ALU.mult))
        add("vector", lambda e, i: e.tensor_copy(tb_i[:, :, :], sidx[:, 1:3, :]))
        add("sync_dma", lambda e, i: e.dma_start(block_dram.rearrange("(c p) -> p c", p=P), tb_i[:, 1, :],
                                                   allow_slow_non_contiguous=True))
        add("sync_dma", lambda e, i: e.dma_start(blk[:, :], block_dram.rearrange("(a s) -> a s", a=1)))
        for c in range(SC):
            for of, to in ((e_rows, dst_r), (s_rows, src_r)):
                add("pool_dma", lambda e, i, c=c, of=of, to=to: e.indirect_dma_start(
                    out=to[:, c, :], out_offset=None, in_=of,
                    in_offset=bass.IndirectOffsetOnAxis(ap=tb_i[:, 0, c:c + 1], axis=0)))
        add("vector", lambda e, i: e.tensor_copy(dst_f, dst_r))
        add("vector", lambda e, i: e.tensor_copy(src_f, src_r))
        add("vector", lambda e, i: e.memset(last_r[:, :, P - 1:P], 1.0))
        add("vector", lambda e, i: e.memset(first_r[:, :, 0:1], -BIG))
        add("vector", lambda e, i: e.tensor_tensor(last_r[:, :, 0:P - 1], dst_f[:, :, 0:P - 1],
                                                   dst_f[:, :, 1:P], ALU.not_equal))
        add("vector", lambda e, i: e.tensor_scalar(first_r[:, :, 1:P], last_r[:, :, 0:P - 1], -BIG, None,
                                                   ALU.mult))
        add("vector", lambda e, i: e.tensor_tensor(dst_f, dst_f, sidx[:, 3, :].unsqueeze(2).to_broadcast([P, SC, P]),
                                                   ALU.subtract))
        for h, fd in first_drams.items():
            for k in range(h):
                add("sync_dma", lambda e, i, h=h, k=k, fd=fd: e.dma_start(
                    fd.rearrange("(c s h) e -> s h c e", s=P, h=h)[:, k], first_r))

        def turn(of):
            def _(e, i):
                for c in range(SC):
                    ins = e.transpose(psT[:, c, :], of[:, c, :], ident[:, :])
                return ins
            return _
        psTs = psT[:, 0:SC, :].rearrange("p c s -> p (c s)")
        for of, to in ((src_f, srcT), (dst_f, slotT), (last_r, lastT)):
            add("tensor", turn(of))
            add("vector", lambda e, i, to=to: e.tensor_copy(to[:, :], psTs))

        WT0, WTE, WTN = wbuf[:, 0, 0:D], wbuf[:, 0, D:3 * D], wbuf[:, 0, 3 * D:4 * D]
        WG = [wbuf[:, 1, 0:D + 2 * HEADS1], wbuf[:, 1, 2 * D:3 * D + 2 * HEADS1]]
        WX = wbuf[:, 2, :]
        w1t = wbuf[:, 3, 0:D]
        w2t = wbuf[:, 3, D:2 * D]

        def turn_w(e, i):
            for k, slot in enumerate((W0, WEA, WEB, WN, W1R, W2R)):
                ins = e.transpose(psT[:, k, :], wraw[:, slot, :], ident[:, :])
            return ins
        add("tensor", turn_w)
        add("vector", lambda e, i: e.tensor_copy(wbuf[:, 0, :].rearrange("p (k f) -> p k f", f=D), psT[:, 0:4, :]))
        add("vector", lambda e, i: e.tensor_copy(wbuf[:, 3, 0:2 * D].rearrange("p (k f) -> p k f", f=D), psT[:, 4:6, :]))

        def w_by_a(e, i):
            for k, wt in enumerate((w1t, w2t)):
                ins = e.matmul(psS[:, 64 * k:64 * k + 2 * HEADS1], wt,
                               adiag[:, 2 * k:2 * k + 2, :].rearrange("p a h -> p (a h)"), start=True, stop=True)
            return ins
        add("tensor", w_by_a)
        for k, slot in enumerate((W1R, W2R)):
            add("vector", lambda e, i, k=k: e.tensor_copy(WG[k][:, D:D + 2 * HEADS1], psS[:, 64 * k:64 * k + 2 * HEADS1]))
            add("vector", lambda e, i, k=k, slot=slot: e.tensor_copy(WG[k][:, 0:D], wraw[:, slot, :]))
        for k, slot in enumerate((WKR, WVR, WQR, WSR)):
            add("vector", lambda e, i, k=k, slot=slot: e.tensor_copy(WX[:, k * D:(k + 1) * D], wraw[:, slot, :]))
        add("vector", lambda e, i: e.memset(acc[:, :, :], 0.0))
        add("vector", lambda e, i: e.memset(GT[:, :, :, D:D + 1], 1.0))
        chain(st_)
        own.close(SC - 1)

        DH = D + HEADS1

        def at(t, i):
            return t[:, bass.ds(i * G, G), :]

        def const(k, n):
            return consts[:, k:k + 1, :].to_broadcast([P, G, n])

        def wide(ap, n):
            return ap.unsqueeze(len(ap.shape)).to_broadcast([*ap.shape, n])

        def heads(ap, h):
            return ap.rearrange("p g (h c) -> p g h c", h=h)

        def node_phase(stages, table=None, rows_of=None):
            if table is not None:
                stages = stages + [("sync_dma", lambda e, i: e.dma_start(
                    at(table.rearrange("(b p) f -> p b f", p=P), i), rows_of[:, :, 0:table.shape[1]]))]
            chain(stages, NBAT)

        def norm_stages():
            mean, var, dev = st[:, 0, 0:G], st[:, 1, 0:G], st[:, 2, 0:G]
            return [
                ("vector", lambda e, i: e.tensor_reduce(mean, at(X, i), AX.X, ALU.add)),
                ("vector", lambda e, i: e.tensor_scalar(mean, mean, 1.0 / D, None, ALU.mult)),
                ("vector", lambda e, i: e.tensor_tensor(Y[:, :, :], at(X, i), wide(mean, D), ALU.subtract)),
                ("scalar", lambda e, i: e.activation(Y2[:, :, :], Y[:, :, :], ACT.Square)),
                ("vector", lambda e, i: e.tensor_reduce(var, Y2[:, :, :], AX.X, ALU.add)),
                ("vector", lambda e, i: e.tensor_scalar(var, var, 1.0 / D, LN_EPS, ALU.mult, ALU.add)),
                ("scalar", lambda e, i: e.activation(dev, var, ACT.Sqrt)),
                ("vector", lambda e, i: e.reciprocal(var, dev)),
                ("vector", lambda e, i: e.scalar_tensor_tensor(
                    out=Y[:, :, :], in0=Y[:, :, :], scalar=0.0, in1=wide(var, D), op0=ALU.max, op1=ALU.mult)),
            ]

        def turn_stages():
            def turn_y(e, i):
                for g in range(G):
                    ins = e.transpose(psT[:, g, :], Y[:, g, :], ident[:, :])
                return ins
            return [("tensor", turn_y), ("scalar", lambda e, i: e.copy(YT[:, :, :], psT[:, :, :]))]

        def product(w):
            def mm(e, i):
                for g in range(G):
                    ins = e.matmul(psD[:, g, 0:w.shape[1]], YT[:, g, :], w, start=True, stop=True)
                return ins
            return ("tensor", mm)

        def plus_bias(to, k):
            return ("vector", lambda e, i: e.tensor_tensor(
                to(i), psD[:, :, :], bias[:, k:k + 1, :].to_broadcast([P, G, D]), ALU.add))

        def x_plus(y):
            return ("vector", lambda e, i: e.tensor_tensor(at(X, i), at(X, i), y, ALU.add))

        def clear_acc():
            return ("vector", lambda e, i: e.tensor_copy(at(acc, i), const(0, DH)))

        def mean_stages(w, k, relu):
            out_ = [
                ("vector", lambda e, i: e.tensor_tensor(Y[:, :, :], at(acc, i)[:, :, 0:D], wide(st[:, 0, 0:G], D), ALU.mult)),
                clear_acc(), *turn_stages(), product(w), plus_bias(lambda i: Y[:, :, :], k),
            ]
            if relu:
                return out_ + [("vector", lambda e, i: e.scalar_tensor_tensor(
                    out=at(X, i), in0=Y[:, :, :], scalar=0.0, in1=at(X, i), op0=ALU.max, op1=ALU.add))]
            return out_ + [x_plus(Y[:, :, :])]

        def softmax_stages(h, op, eps):
            sums = lambda i: at(acc, i)[:, :, 0:D + h].rearrange("p g (h c) -> p g h c", h=h)
            c = D // h
            den = st[:, 0, 0:G * h].rearrange("p (g h) -> p g h", h=h)
            den4 = den.unsqueeze(3)
            return [
                ("vector", lambda e, i: e.tensor_scalar(den4, sums(i)[:, :, :, c:c + 1], eps, None, op)),
                ("vector", lambda e, i: e.reciprocal(den, den)),
                ("vector", lambda e, i: e.tensor_tensor(heads(Y[:, :, :], h), sums(i)[:, :, :, 0:c], wide(den, c), ALU.mult)),
            ]

        def gat_stages(wg):
            d0 = D + HEADS1
            s4 = lambda i: at(acc, i).rearrange("p g (h c) -> p g h c", h=HEADS1)
            c = D // HEADS1
            return [
                product(wg[:, 0:D]),
                ("scalar", lambda e, i: e.copy(R[:, :, 0:D], psD[:, :, :])),
                product(wg[:, D:D + 2 * HEADS1]),
                ("vector", lambda e, i: e.tensor_copy(R[:, :, D:d0], psD[:, :, 0:HEADS1])),
                ("vector", lambda e, i: e.tensor_copy(at(nodeD, i), psD[:, :, HEADS1:2 * HEADS1])),
                ("vector", lambda e, i: e.tensor_tensor(Y2[:, :, 0:HEADS1], R[:, :, D:d0], at(nodeD, i), ALU.add)),
                ("vector", lambda e, i: e.scalar_tensor_tensor(
                    out=at(nodeM, i), in0=Y2[:, :, 0:HEADS1], scalar=0.2, in1=Y2[:, :, 0:HEADS1],
                    op0=ALU.mult, op1=ALU.max)),
                ("vector", lambda e, i: e.tensor_copy(at(acc, i), const(1, DH))),
                ("vector", lambda e, i: e.tensor_copy(s4(i)[:, :, :, 0:c], heads(R[:, :, 0:D], HEADS1))),
            ]

        signals = {}

        def signal(name, per=1):
            signals[name] = Signal(sem(name), per)
            return signals[name]

        names = ("index", "onehot", "turned", "onehotT", "toedge", "prod", "head", "logit", "logitT", "seg",
                 "segT", "nmax", "pen", "tmax", "drop", "resc", "maxedge", "below", "bound", "weight",
                 "values", "sums")
        for n in names:
            signal(n)
        for n, per in (("lastmax", 2), ("diff", G), ("upd", G), ("scaled", G), ("added", G)):
            signal(n, per)
        ring_rows = [Signal(sem(f"rows{r}"), 1, 16 * G) for r in range(RING)]
        ring_first = [Signal(sem(f"first{r}"), 1, 16) for r in range(RING)]
        with nc.Block() as block:
            @block.gpsimd
            def _(eng):
                for sg in signals.values():
                    sg.base = RING * sg.per
                    eng.sem_inc(sg.sem, sg.base)

        srcI = sb("srcI", [P, RING, G], I32)

        def edge_pass(kind, table, h=0):
            W = table.shape[1]
            soft = kind in ("gat", "dot")
            VW = {"sum": D + 1, "mlp": D}.get(kind, D + h)
            HG = h * G
            C = D // h if soft else 0
            used = set()
            maxima = psS[:, 256:256 + G * (h + 1)].rearrange("p (g w) -> p g w", g=G)
            edge_max = psS[:, 0:HG].rearrange("p (g h) -> p g h", g=G)

            def by_head(ap):
                return ap.rearrange("p (g h) -> p g h", g=G)

            def wait(name, eng, g, k=None):
                signals[name].wait(eng, g, k)

            def done(name, ins):
                used.add(name)
                signals[name].done(ins)

            def at_block(t, b, w):
                return t[:, bass.ds(b, 1), 0:w].rearrange("p o w -> p (o w)")

            def pool(eng, i, k):
                g = i * RING + k
                wait({"sum": "sums", "mlp": "prod"}.get(kind, "values"), eng, g - RING)
                wait("index", eng, g)
                table_ready(eng)
                apart(eng)
                for j in range(G):
                    eng.indirect_dma_start(
                        out=GT[:, k, j, 0:W], out_offset=None, in_=table,
                        in_offset=bass.IndirectOffsetOnAxis(ap=srcI[:, k, j:j + 1], axis=0),
                    ).then_inc(ring_rows[k].sem, 16)

            def sync(eng, i, k):
                g = i * RING + k
                wait("seg", eng, g - RING)
                ring_first[k].done(eng.dma_start(first[0:HG, k, :], first_drams[h][bass.ds(g * HG, HG), :]))

            def act_index(eng, i, k):
                g = i * RING + k
                if not (isinstance(i, int) and i == 0):
                    ring_rows[k].wait(eng, i - 1)
                done("index", eng.copy(srcI[:, k, :], srcT[:, bass.ds(g * G, G)]))

            def act_A(eng, i, k):
                g = i * RING + k
                q = k % 2
                if kind == "sum":
                    return
                wait("turned", eng, g)
                wait("maxedge" if soft else "toedge", eng, g - 2)
                done("onehotT", eng.copy(Ot[:, q, :, :], psT[:, :, :]))

            def act_A1(eng, i, k):
                g = i * RING + k
                if kind == "mlp":
                    wait("prod", eng, g)
                    wait("sums", eng, g - 2)
                    done("values", eng.activation(V[:, k % 2, :, 0:D], prod[:, :, :], ACT.Relu))

            def act_B(eng, i, k):
                g = i * RING + k
                q = k % 2
                if soft:
                    wait("drop", eng, g)
                    wait("added", eng, g - 2)
                    done("resc", eng.activation(resc[:, q, :, 0:h], diff[:, q, :, 0:h], ACT.Exp))
                    wait("bound", eng, g)
                    wait("sums", eng, g - 2)
                    v = V[:, q, :, 0:D + h].rearrange("p g (h c) -> p g h c", h=h)
                    done("weight", eng.activation(v[:, :, :, C:C + 1], by_head(below[:, q, 0:HG]).unsqueeze(3), ACT.Exp))

            pe_b = {}

            def pe_A0(eng, i, k):
                g = i * RING + k
                if kind == "sum":
                    return
                wait("onehot", eng, g)
                wait("onehotT", eng, g - 1)
                for j in range(G):
                    ins = eng.transpose(psT[:, j, :], O[:, k % 2, j, :], ident[:, :])
                done("turned", ins)

            def pe_A1(eng, i, k):
                g = i * RING + k
                if kind == "sum":
                    return
                pe_b[k % 2] = blocks_of(eng, g, k % 2)
                wait("onehotT", eng, g)
                wait("prod", eng, g - 1)
                tab, w = (nodeD, h) if kind == "gat" else (nodeQ, D)
                for j in range(G):
                    ins = eng.matmul(psD[:, j, 0:w], Ot[:, k % 2, j, :], at_block(tab, pe_b[k % 2][j], w),
                                     start=True, stop=True)
                done("toedge", ins)

            def pe_A2(eng, i, k):
                g = i * RING + k
                if soft:
                    wait("logit", eng, g)
                    wait("below", eng, g - 1)
                    done("logitT", eng.transpose(psS[0:HG, 0:P], lg[:, k % 2, 0:HG], ident[:, :]))

            def pe_A3(eng, i, k):
                g = i * RING + k
                if soft:
                    wait("seg", eng, g)
                    if HG < P:
                        apart(eng)
                    done("segT", eng.transpose(psS[:, P:P + HG], seg[0:HG, k % 2, :], ident[0:HG, 0:HG]))

            def pe_B0(eng, i, k):
                g = i * RING + k
                if soft:
                    wait("lastmax", eng, g)
                    for j in range(G):
                        ins = eng.matmul(maxima[:, j, :], O[:, k % 2, j, :], lastmax[:, k % 2, j, 0:h + 1],
                                         start=True, stop=True)
                    done("nmax", ins)

            def pe_B1(eng, i, k):
                g = i * RING + k
                if soft:
                    wait("upd", eng, g)
                    if k == 0:
                        pe_b[0] = blocks_of(eng, g, 0)
                    for j in range(G):
                        ins = eng.matmul(edge_max[:, j, :], Ot[:, k % 2, j, :], at_block(nodeM, pe_b[k % 2][j], h),
                                         start=True, stop=True)
                    done("maxedge", ins)

            def pe_B2(eng, i, k):
                g = i * RING + k
                if kind == "sum":
                    ring_rows[k].wait(eng, i)
                    wait("onehot", eng, g)
                else:
                    wait("values", eng, g)
                wait("added", eng, g - 1)
                for j in range(G):
                    val = GT[:, k, j, 0:VW] if kind == "sum" else V[:, k % 2, j, 0:VW]
                    ins = eng.matmul(agg(j, VW), O[:, k % 2, j, :], val, start=True, stop=True)
                done("sums", ins)

            def dve_A0(eng, i, k):
                g = i * RING + k
                wait("sums", eng, g - 2)
                done("onehot", eng.tensor_tensor(
                    O[:, k % 2, :, :], iota[:, :].unsqueeze(1).to_broadcast([P, G, P]),
                    wide(slotT[:, bass.ds(g * G, G)], P), ALU.is_equal))

            def dve_A1(eng, i, k):
                g = i * RING + k
                q = k % 2
                if kind == "sum":
                    return
                ring_rows[k].wait(eng, i)
                wait("toedge", eng, g)
                if kind == "mlp":
                    wait("values", eng, g - 1)
                    done("prod", eng.tensor_tensor(prod[:, :, :], psD[:, :, :], GT[:, k, :, 0:D], ALU.add))
                    return
                if kind == "gat":
                    done("prod", eng.tensor_tensor(by_head(lg2[:, 0:HG]), psD[:, :, 0:h], GT[:, k, :, D:D + h], ALU.add))
                    wait("prod", eng, g)
                    wait("below", eng, g - 2)
                    done("logit", eng.scalar_tensor_tensor(
                        out=lg[:, q, 0:HG], in0=lg2[:, 0:HG], scalar=0.2, in1=lg2[:, 0:HG],
                        op0=ALU.mult, op1=ALU.max))
                    return
                done("prod", eng.tensor_tensor(prod[:, :, :], psD[:, :, :], GT[:, k, :, 0:D], ALU.mult))
                wait("prod", eng, g)
                done("head", eng.tensor_reduce(lg2[:, 0:HG], prod[:, :, :].rearrange("p g (h c) -> p (g h) c", h=h),
                                               AX.X, ALU.add))
                wait("head", eng, g)
                wait("below", eng, g - 2)
                done("logit", eng.tensor_scalar(lg[:, q, 0:HG], lg2[:, 0:HG], float(C) ** -0.5, None, ALU.mult))

            def dve_A2(eng, i, k):
                g = i * RING + k
                if soft:
                    wait("logitT", eng, g)
                    ring_first[k].wait(eng, i)
                    wait("segT", eng, g - 2)
                    done("seg", eng.tensor_tensor_scan(seg[0:HG, k % 2, :], first[0:HG, k, :], psS[0:HG, 0:P],
                                                       -BIG, ALU.add, ALU.max))

            def dve_A3(eng, i, k):
                g = i * RING + k
                if soft:
                    wait("segT", eng, g)
                    wait("nmax", eng, g - 2)
                    last = lastT[:, bass.ds(g * G, G)]
                    done("lastmax", eng.tensor_tensor(lastmax[:, k % 2, :, 0:h], by_head(psS[:, P:P + HG]),
                                                      wide(last, h), ALU.mult))
                    done("lastmax", eng.tensor_copy(lastmax[:, k % 2, :, h:h + 1], last.unsqueeze(2)))

            dve_b = {}

            def dve_B0(eng, i, k):
                g = i * RING + k
                q = k % 2
                dve_b[q] = blocks_of(eng, g, q)
                if not soft:
                    return
                wait("nmax", eng, g)
                done("pen", eng.tensor_scalar(pen[:, q, :].unsqueeze(2), maxima[:, :, h:h + 1], BIG, -BIG, ALU.mult, ALU.add))
                wait("pen", eng, g)
                done("tmax", eng.tensor_tensor(tmax[:, q, :, 0:h], maxima[:, :, 0:h], wide(pen[:, q, :], h), ALU.add))
                wait("tmax", eng, g)
                wait("maxedge", eng, g - 1)
                wait("resc", eng, g - 2)
                for j in range(G):
                    m = at_block(nodeM, dve_b[q][j], h)
                    if j:
                        wait("upd", eng, g, j - 1)
                    done("diff", eng.tensor_tensor(diff[:, q, j, 0:h], m, tmax[:, q, j, 0:h], ALU.subtract))
                    wait("diff", eng, g, j)
                    done("upd", eng.tensor_tensor(m, m, tmax[:, q, j, 0:h], ALU.max))
                done("drop", eng.tensor_scalar(diff[:, q, :, 0:h], diff[:, q, :, 0:h], 0.0, None, ALU.min))

            def dve_B1(eng, i, k):
                g = i * RING + k
                q = k % 2
                if soft:
                    wait("maxedge", eng, g)
                    wait("weight", eng, g - 2)
                    done("below", eng.tensor_tensor(by_head(below[:, q, 0:HG]), by_head(lg[:, q, 0:HG]), edge_max,
                                                    ALU.subtract))
                    wait("below", eng, g)
                    done("bound", eng.tensor_scalar(below[:, q, 0:HG], below[:, q, 0:HG], 0.0, None, ALU.min))

            def dve_B2(eng, i, k):
                g = i * RING + k
                if soft:
                    wait("weight", eng, g)
                    f0 = 0 if kind == "gat" else D
                    v = V[:, k % 2, :, 0:D + h].rearrange("p g (h c) -> p g h c", h=h)
                    done("values", eng.tensor_tensor(
                        v[:, :, :, 0:C], heads(GT[:, k, :, f0:f0 + D], h),
                        v[:, :, :, C:C + 1].to_broadcast([P, G, h, C]), ALU.mult))

            def dve_B3(eng, i, k):
                g = i * RING + k
                q = k % 2
                if k == RING - 1:
                    dve_b[q] = blocks_of(eng, g, q)
                wait("sums", eng, g)
                if soft:
                    wait("resc", eng, g)
                sums_of = [at_block(acc, b, VW) for b in dve_b[q]]
                wait("added", eng, g - 1)
                if soft:
                    for j, a in enumerate(sums_of):
                        ah = a.rearrange("p (h c) -> p h c", h=h)
                        if j:
                            wait("scaled", eng, g, j - 1)
                        done("scaled", eng.tensor_tensor(ah, ah, wide(resc[:, q, j, 0:h], C + 1), ALU.mult))
                    wait("scaled", eng, g)
                for j, a in enumerate(sums_of):
                    if j:
                        wait("added", eng, g, j - 1)
                    done("added", eng.tensor_tensor(a, a, agg(j, VW), ALU.add))

            ORDER = {
                "tensor": (("A", pe_A0), ("B", pe_B0), ("A", pe_A1), ("B", pe_B1), ("A", pe_A2), ("A", pe_A3),
                           ("B", pe_B2)),
                "vector": (("A", dve_A0), ("C", dve_B3), ("B", dve_B0), ("A", dve_A1), ("B", dve_B1), ("A", dve_A2),
                           ("B", dve_B2), ("A", dve_A3)),
                "scalar": (("I", act_index), ("A", act_A), ("A", act_A1), ("B", act_B)),
            }

            def run(key, eng):
                parts = ORDER[key]

                def turn_(i, k, which="ABCI"):
                    nxt = (i, k + 1) if k + 1 < RING else (i + 1, 0)
                    prv = (i, k - 1) if k else (i - 1, RING - 1)
                    for what, fn in parts:
                        if what in which:
                            fn(eng, *{"A": nxt, "B": (i, k), "C": prv, "I": (i, k)}[what])

                last = NG // RING - 1
                if key == "scalar":
                    def turn_(i, k, which="ABI"):
                        nxt = (i, k + 1) if k + 1 < RING else (i + 1, 0)
                        if "A" in which:
                            act_A(eng, *nxt)
                        if "I" in which:
                            act_index(eng, i + 1, k)
                        if "A" in which:
                            act_A1(eng, *nxt)
                        if "B" in which:
                            act_B(eng, i, k)
                    for k in range(RING):
                        act_index(eng, 0, k)
                    act_A(eng, 0, 0)
                    act_A1(eng, 0, 0)
                    with eng.Fori(0, last) as i:
                        for k in range(RING):
                            turn_(i, k)
                    for k in range(RING):
                        turn_(last, k, "AB" if k < RING - 1 else "B")
                    return
                for what, fn in parts:
                    if what == "A":
                        fn(eng, 0, 0)
                for k in range(RING):
                    turn_(0, k, "ABC" if k else "AB")
                with eng.Fori(1, last) as i:
                    for k in range(RING):
                        turn_(i, k)
                for k in range(RING):
                    turn_(last, k, "ABC" if k < RING - 1 else "BC")
                for what, fn in parts:
                    if what == "C":
                        fn(eng, last, RING - 1)

            with nc.Block() as block:
                @block.gpsimd
                def _(eng):
                    with eng.Fori(0, NG // RING) as i:
                        for k in range(RING):
                            pool(eng, i, k)

                @block.sync
                def _(eng):
                    if soft:
                        with eng.Fori(0, NG // RING) as i:
                            for k in range(RING):
                                sync(eng, i, k)

                @block.scalar
                def _(eng):
                    run("scalar", eng)

                @block.tensor
                def _(eng):
                    run("tensor", eng)

                @block.vector
                def _(eng):
                    run("vector", eng)

            for n in used:
                signals[n].close(NG)
            for r in ring_rows + (ring_first if soft else []):
                r.close(NG // RING)

        def table_ready(eng):
            eng.wait_ge(chain_sems["sync_dma"].sem, chain_sems["sync_dma"].base)

        reg_sets = {}

        def blocks_of(eng, g, q):
            if (eng.engine, q) not in reg_sets:
                reg_sets[eng.engine, q] = [eng.alloc_register(f"block_{q}_{j}") for j in range(G)]
            regs = reg_sets[eng.engine, q]
            eng.load(regs, blk[0:1, bass.ds(g * G, G)])
            return [eng.snap(r, min_val=0, max_val=NB - 1) for r in regs]

        T0, T1, T2, T3, T4 = tables
        node_phase(norm_stages(), T0, Y)
        edge_pass("sum", T0)

        recip = ("vector", lambda e, i: e.reciprocal(st[:, 0, 0:G], st[:, 1, 0:G]))
        node_phase([
            ("vector", lambda e, i: e.tensor_copy(at(deg, i), at(acc, i)[:, :, D:D + 1])),
            ("vector", lambda e, i: e.tensor_scalar(st[:, 1, 0:G].unsqueeze(2), at(deg, i), MEAN_EPS, None, ALU.add)),
            recip, *mean_stages(WT0, 0, False), *norm_stages(), *turn_stages(),
            product(WTE[:, 0:D]), ("scalar", lambda e, i: e.copy(R[:, :, 0:D], psD[:, :, :])),
            product(WTE[:, D:2 * D]), ("vector", lambda e, i: e.tensor_copy(at(nodeQ, i), psD[:, :, :])),
        ], T1, R)
        edge_pass("mlp", T1)

        node_phase([
            ("vector", lambda e, i: e.tensor_scalar(st[:, 1, 0:G].unsqueeze(2), at(deg, i), 1.0, None, ALU.max)),
            recip, *mean_stages(WTN, 1, True), *norm_stages(), *turn_stages(), *gat_stages(WG[0]),
        ], T2, R)
        edge_pass("gat", T2, HEADS1)

        node_phase([
            *softmax_stages(HEADS1, ALU.add, SOFTMAX_EPS),
            ("vector", lambda e, i: e.tensor_tensor(Y[:, :, :], Y[:, :, :], bias[:, 2:3, :].to_broadcast([P, G, D]), ALU.add)),
            ("vector", lambda e, i: e.tensor_scalar(Y2[:, :, :], Y[:, :, :], 0.0, None, ALU.min)),
            ("scalar", lambda e, i: e.activation(Y2[:, :, :], Y2[:, :, :], ACT.Exp)),
            ("vector", lambda e, i: e.tensor_scalar(Y2[:, :, :], Y2[:, :, :], -1.0, None, ALU.add)),
            ("vector", lambda e, i: e.scalar_tensor_tensor(out=Y[:, :, :], in0=Y[:, :, :], scalar=0.0,
                                                           in1=Y2[:, :, :], op0=ALU.max, op1=ALU.add)),
            *turn_stages(), *gat_stages(WG[1]),
        ], T3, R)
        edge_pass("gat", T3, HEADS1)

        node_phase([
            *softmax_stages(HEADS1, ALU.add, SOFTMAX_EPS),
            ("vector", lambda e, i: e.tensor_tensor(Y[:, :, :], Y[:, :, :], bias[:, 3:4, :].to_broadcast([P, G, D]), ALU.add)),
            x_plus(Y[:, :, :]), clear_acc(), ("vector", lambda e, i: e.tensor_copy(at(nodeM, i), const(2, HEADS1))),
            *norm_stages(), *turn_stages(),
            product(WX[:, 0:D]), plus_bias(lambda i: R[:, :, 0:D], 4),
            product(WX[:, D:2 * D]), plus_bias(lambda i: R[:, :, D:2 * D], 5),
            product(WX[:, 2 * D:3 * D]), plus_bias(lambda i: at(nodeQ, i), 6),
            product(WX[:, 3 * D:4 * D]), plus_bias(lambda i: Y[:, :, :], 7), x_plus(Y[:, :, :]),
        ], T4, R)
        edge_pass("dot", T4, HEADS3)

        node_phase([*softmax_stages(HEADS3, ALU.max, SOFTMAX_EPS), x_plus(Y[:, :, :])])
        chain([
            ("sync_dma", lambda e, i: e.dma_start(out[0:FULL * P, :].rearrange("(b p) f -> p b f", p=P), X[:, 0:FULL, :])),
            ("sync_dma", lambda e, i: e.dma_start(out[FULL * P:N, :], X[0:REST, FULL, :])),
        ])
        with nc.Block() as block:
            @block.sync
            def _(eng):
                table_ready(eng)


INPUTS = ["x", "src", "dst", "L0_gnn_W", "L0_gnn_b", "L1_gnn_W_edge", "L1_gnn_W_node", "L1_gnn_b_node",
          "L2_gnn_W1", "L2_gnn_a_src1", "L2_gnn_a_dst1", "L2_gnn_b1", "L2_gnn_W2", "L2_gnn_a_src2",
          "L2_gnn_a_dst2", "L2_gnn_b2", "L3_gnn_Wq", "L3_gnn_bq", "L3_gnn_Wk", "L3_gnn_bk", "L3_gnn_Wv",
          "L3_gnn_bv", "L3_gnn_Wskip", "L3_gnn_bskip"]


def kernel(**inputs):
    import numpy as np
    from concourse import bacc
    from concourse.bass_utils import run_bass_kernel_spmd

    nc = bacc.Bacc("TRN2", target_bir_lowering=False, num_devices=1)
    arrays, args = {}, []
    for name in INPUTS:
        a = np.ascontiguousarray(inputs[name])
        arrays[f"in_{name}"] = a
        args.append(nc.dram_tensor(f"in_{name}", a.shape, mybir.dt.from_np(a.dtype), kind="ExternalInput").ap())
    shape = inputs["x"].shape
    out = nc.dram_tensor("out", shape, F32, kind="ExternalOutput").ap()
    program(nc, *args, out)
    r = run_bass_kernel_spmd(nc, [arrays], core_ids=[0])
    return r.results[0]["out"]
```

```python
from contextlib import ExitStack

import concourse.bass as bass
from concourse import mybir

F32 = mybir.dt.float32
BF16 = mybir.dt.bfloat16
I32 = mybir.dt.int32
ALU = mybir.AluOpType
ACT = mybir.ActivationFunctionType
AX = mybir.AxisListType

P = 128
G = 8
Q = 4
RING = 4
BIG = 1.0e30
LN_EPS = 1e-5
MEAN_EPS = 1e-6
SOFTMAX_EPS = 1e-16


class Signal:

    def __init__(self, sem, per=1, by=1):
        self.sem, self.per, self.by, self.base = sem, per, by, 0

    def done(self, ins):
        ins.then_inc(self.sem, self.by)

    def value(self, rnd, k=None):
        k = self.per if k is None else k + 1
        return (rnd * self.per + k) * self.by + self.base

    def wait(self, eng, rnd, k=None):
        v = self.value(rnd, k)
        if not isinstance(v, int) or v > self.base:
            eng.wait_ge(self.sem, v)

    def close(self, rounds):
        self.base += rounds * self.per * self.by


def program(nc, x, src, dst, w0, b0, w_edge, w_node, b_node, w1, as1, ad1, b1, w2, as2, ad2, b2,
            wq, bq, wk, bk, wv, bv, wskip, bskip, out):
    N, D = x.shape
    E = src.shape[0]
    T = -(-E // P)
    NB = -(-N // P)
    NP = NB * P
    STEPS = T + NB - 1
    NG = -(-STEPS // G)
    SC = -(-(NG * G) // P)
    SP_ = SC * P
    QS = G // Q
    NGQ = -(-((STEPS + NB * (Q - 1)) // Q) // QS)
    SCQ = -(-(NGQ * G) // P)
    FULL, REST = N // P, N % P
    NBAT = NB // G
    HEADS1, HEADS3 = as1.shape[0], 2
    assert D == P and NB % G == 0 and REST and NG * G == STEPS and NG % RING == 0

    first_drams = {h: nc.dram_tensor(f"first_dram{h}", [SCQ * P * h, P], F32, kind="Internal").ap()
                   for h in (as1.shape[0], 2)}
    dst_pad = nc.dram_tensor("dst_pad", [(T + 1) * P], I32, kind="Internal").ap()
    src_pad = nc.dram_tensor("src_pad", [(T + 1) * P], I32, kind="Internal").ap()
    block_drams = [nc.dram_tensor(f"block_dram{k}", [c * P], I32, kind="Internal").ap() for k, c in enumerate((SC, SCQ))]
    tables = [nc.dram_tensor(f"table{i}", [NP, w], F32, kind="Internal").ap()
              for i, w in enumerate((D, D, D + HEADS1, D + HEADS1, 2 * D))]

    ctx = ExitStack()
    with ctx:
        def sb(name, shape, dt=F32):
            return ctx.enter_context(nc.sbuf_tensor(name, shape, dt))

        def sem(name):
            return ctx.enter_context(nc.semaphore(name))

        X = sb("X", [P, NB, D])
        acc = sb("acc", [P, NB + G, D + HEADS1])
        nodeQ = sb("nodeQ", [P, NB, 3, D], BF16)
        nodeD = sb("nodeD", [P, NB, 3, HEADS1], BF16)
        nodeM = sb("nodeM", [P, NB, HEADS1])
        deg = sb("deg", [P, NB, 1])
        srcT = [sb(f"srcT{k}", [P, c * P], I32) for k, c in enumerate((SC, SCQ))]
        slotT = [sb(f"slotT{k}", [P, c * P], BF16) for k, c in enumerate((SC, SCQ))]
        lastT = sb("lastT", [P, SCQ * P], BF16)
        blkq = sb("blkq", [1, SCQ * P // Q], I32)
        fresh = sb("fresh", [P, SCQ * P // Q])
        blk = sb("blk", [1, SP_], I32)
        blk_rel = sb("blk_rel", [1, SP_], I32)
        ident = sb("ident", [P, P])
        iota = sb("iota", [P, P])
        identb = sb("identb", [P, P], BF16)
        iotab = sb("iotab", [P, P], BF16)
        zerob = sb("zerob", [1, 512], BF16)
        GT = sb("GT", [P, RING, G, 2 * D])
        consts = sb("consts", [P, 3, 1])
        wbuf = sb("wbuf", [P, 3, 4 * D])
        bias = sb("bias", [P, 9, D])
        O = sb("O", [P, 2, G, P])
        Ob = sb("Ob", [P, RING, G, P], BF16)
        Ot = sb("Ot", [P, RING, G, P], BF16)
        V = sb("V", [P, 2, G, D + HEADS1])
        prod = sb("prod", [P, G, D])
        lg = sb("lg", [P, 2, G * HEADS1])
        lg2 = sb("lg2", [P, G * HEADS1])
        first = sb("first", [P, RING, P])
        seg = sb("seg", [P, 2, P])
        lastmax = sb("lastmax", [P, 2, G, HEADS1 + 1])
        lastmax1 = sb("lastmax1", [P, 2, G, HEADS1 + 1])
        lastmax2 = sb("lastmax2", [P, 2, G, HEADS1 + 1], BF16)
        tmax = sb("tmax", [P, 2, G, HEADS1])
        pen = sb("pen", [P, 2, G])
        qmax = sb("qmax", [P, 2, QS, HEADS1])
        oldM = sb("oldM", [P, 2, QS, HEADS1])
        newM = sb("newM", [P, 2, QS, HEADS1])
        newM1 = sb("newM1", [P, 2, QS, HEADS1])
        newM2 = sb("newM2", [P, 2, QS, HEADS1], BF16)
        diff = sb("diff", [P, 2, QS, HEADS1])
        resc = sb("resc", [P, 2, QS, HEADS1])
        below = sb("below", [P, 2, G * HEADS1])
        Y, Y2, YT = O[:, 0], O[:, 1], prod
        R = GT[:, 0, :, :]
        st = sb("st", [P, 4, G * HEADS1])

        psT = ctx.enter_context(nc.psum_tensor("psT", [P, G, P], BF16))
        psD = ctx.enter_context(nc.psum_tensor("psD", [P, G, P], F32))
        psS = ctx.enter_context(nc.psum_tensor("psS", [P, 512], F32))
        psA = ctx.enter_context(nc.psum_tensor("psA", [P, G, 256], F32))
        psN = psA[:, 0:G // 2, :].rearrange("p a (b e) -> p (a b) e", e=P)

        def top(ap):
            return ap.bitcast(BF16)[..., 1::2]

        apart_sem = sem("apart")

        def apart(eng):
            eng.sem_inc(apart_sem, 1)

        chain_sems = {kind: Signal(sem(f"chain_{kind}"), 0, 16 if kind.endswith("dma") else 1)
                      for kind in ("compute", "sync_dma", "pool_dma")}

        def chain(stages, rounds=1):
            stages = [stage if len(stage) == 3 else (*stage, 1) for stage in stages]
            kinds = [who if who.endswith("dma") else "compute" for who, _, _ in stages]
            places, count = [], dict.fromkeys(chain_sems, 0)
            for kind, (_, _, n) in zip(kinds, stages):
                count[kind] += n
                places.append(count[kind] - 1)
            for kind, sg in chain_sems.items():
                sg.per = count[kind]
            with nc.Block() as block:
                def body(eng, key, i):
                    for n, (who, fn, parts) in enumerate(stages):
                        if who.split("_")[0] != key:
                            continue
                        if n:
                            chain_sems[kinds[n - 1]].wait(eng, i, places[n - 1])
                        elif rounds > 1:
                            sg = chain_sems[kinds[-1]]
                            sg.wait(eng, i - 1)
                        if rounds > 1 and kinds[n] == "compute":
                            apart(eng)
                        sg = chain_sems[kinds[n]]
                        made = fn(eng, i)
                        made = made if isinstance(made, list) else [made]
                        assert len(made) == parts
                        for ins in made:
                            ins.then_inc(sg.sem, sg.by)

                def run(key):
                    def _(eng):
                        if not any(who.split("_")[0] == key for who, _, _ in stages):
                            return
                        if rounds == 1:
                            body(eng, key, 0)
                        else:
                            with eng.Fori(0, rounds) as i:
                                body(eng, key, i)
                    return _

                block.sync(run("sync"))
                block.gpsimd(run("pool"))
                block.scalar(run("scalar"))
                block.vector(run("vector"))
                block.tensor(run("tensor"))
            for sg in chain_sems.values():
                sg.close(rounds)

        load_sem = sem("load")
        c_sem = sem("const")
        zrow, padrow = (acc[0:1, 2 * k:2 * k + 2, 0:P].bitcast(I32) for k in range(2))
        rowi = [t[0:1, :, :].rearrange("p g e -> p (g e)").bitcast(I32) for t in (O[:, 0], O[:, 1], prod)]
        work = nodeQ[:, :, :, :].rearrange("p b k f -> p (b k f)").bitcast(F32)
        vsb = [work[:, k * 1024:(k + 1) * 1024] for k in range(2)]
        row = [work[0:1, k * 1024:(k + 1) * 1024] for k in range(2, 5)]
        vall = psD[:, :, :].rearrange("p a b -> p (a b)")
        sidx_i = sb("sidx_i", [P, SCQ], I32)
        sidx = sb("sidx", [P, 6, SCQ])
        tb_i = sb("tb_i", [P, 2, SCQ], I32)
        bcol = sb("bcol", [P, 6])
        bcol_i = sb("bcol_i", [P, 1], I32)
        tri = sb("tri", [P, NB])
        brow = sb("brow", [P, 2, NB])
        bwork = work[:, 5 * 1024:5 * 1024 + 2 * SCQ * NB].rearrange("p (k c b) -> p k c b", k=2, c=SCQ)
        iota_i = sb("iota_i", [P, P], I32)
        hmask = sb("hmask", [P, HEADS1])
        acol = sb("acol", [P, 4])
        adiag = sb("adiag", [P, 4, HEADS1])
        wraw = V[:, :, :, :].rearrange("p a g e -> p (a g e)")[:, 0:10 * D].rearrange("p (k f) -> p k f", f=D)
        flat = GT[:, :, :, :].rearrange("p r g w -> p (r g w)")
        rows = [flat[:, i * SCQ * P:(i + 1) * SCQ * P].rearrange("p (c e) -> p c e", c=SCQ) for i in range(6)]
        assert 6 * SCQ * P + 2 * 1024 <= RING * G * 2 * D and T <= 1024
        edges_all = [flat[:, 6 * SCQ * P + k * 1024:6 * SCQ * P + k * 1024 + T] for k in range(2)]

        W0, WEA, WEB, WN, W1R, W2R, WQR, WKR, WVR, WSR = range(10)
        n_loads = 0
        with nc.Block() as block:
            @block.sync
            def _(eng):
                n = 0

                def load(to, of):
                    nonlocal n
                    eng.dma_start(to, of).then_inc(load_sem, 16)
                    n += 1

                load(X[:, 0:FULL, :], x[0:FULL * P, :].rearrange("(b p) f -> p b f", p=P))
                for slot, w in ((W0, w0), (WEA, w_edge[:, 0:D]), (WEB, w_edge[:, D:2 * D]),
                                (WN, w_node), (W1R, w1), (W2R, w2), (WQR, wq), (WKR, wk),
                                (WVR, wv), (WSR, wskip)):
                    load(wraw[:, slot, :], w)
                for k, b in enumerate((b0, b_node, b1, b2, bk, bv, bq, bskip)):
                    load(bias[:, k, :], b.rearrange("(a f) -> a f", a=1).to_broadcast([P, D]))
                for k, a in enumerate((as1, ad1, as2, ad2)):
                    load(acol[:, k:k + 1], a.rearrange("h (c o) -> (h c) o", o=1))
                load(dst_pad[0:E].rearrange("(a n) -> a n", a=8), dst.rearrange("(a n) -> a n", a=8))
                load(src_pad[0:E].rearrange("(a n) -> a n", a=8), src.rearrange("(a n) -> a n", a=8))
                eng.wait_ge(c_sem, 3)
                load(X[0:REST, FULL, :], x[FULL * P:N, :])
                load(dst_pad[E:(T + 1) * P].rearrange("(a k n) -> a k n", a=1, k=2), padrow[:, :, 0:((T + 1) * P - E) // 2])
                load(src_pad[E:(T + 1) * P].rearrange("(a k n) -> a k n", a=1, k=2), zrow[:, :, 0:((T + 1) * P - E) // 2])
                eng.wait_ge(load_sem, 16 * n)
                nonlocal n_loads
                n_loads = n

            @block.gpsimd
            def _(eng):
                eng.memset(zrow, 0).then_inc(c_sem, 1)
                eng.memset(padrow, 2 * NP).then_inc(c_sem, 1)
                eng.memset(X[:, FULL, :], 0.0).then_inc(c_sem, 1)
                eng.memset(ident[:, :], 0.0).then_inc(c_sem, 1)
                eng.memset(hmask[:, :], 1.0).then_inc(c_sem, 1)
                eng.memset(tri[:, :], 1.0).then_inc(c_sem, 1)
                for k, value in enumerate((0.0, 1.0, -BIG)):
                    eng.memset(consts[:, k, :], value).then_inc(c_sem, 1)
                eng.wait_ge(c_sem, 9)
                eng.affine_select(out=ident[:, :], in_=ident[:, :], compare_op=ALU.not_equal, fill=1.0,
                                  base=0, pattern=[[-1, P]], channel_multiplier=1).then_inc(c_sem, 1)
                eng.affine_select(out=tri[:, :], in_=tri[:, :], compare_op=ALU.is_ge, fill=0.0,
                                  base=-1, pattern=[[1, NB]], channel_multiplier=-1).then_inc(c_sem, 1)
                eng.affine_select(out=hmask[:, :], in_=hmask[:, :], compare_op=ALU.is_ge, fill=0.0,
                                  base=0, pattern=[[-(D // HEADS1), HEADS1]],
                                  channel_multiplier=1).then_inc(c_sem, 1)
                eng.wait_ge(c_sem, 12)
                eng.affine_select(out=hmask[:, :], in_=hmask[:, :], compare_op=ALU.is_ge, fill=0.0,
                                  base=D // HEADS1 - 1, pattern=[[D // HEADS1, HEADS1]],
                                  channel_multiplier=-1).then_inc(c_sem, 1)
                eng.iota(iota_i[:, :], pattern=[[1, P]], base=0, channel_multiplier=0).then_inc(c_sem, 1)
                eng.iota(sidx_i[:, :], pattern=[[P, SCQ]], base=0, channel_multiplier=1).then_inc(c_sem, 1)
                eng.iota(rowi[2][:, 0:T], pattern=[[1, T]], base=0, channel_multiplier=0).then_inc(c_sem, 1)

            @block.vector
            def _(eng):
                eng.wait_ge(c_sem, 16)
                eng.tensor_copy(iota[:, :], iota_i[:, :]).then_inc(c_sem, 1)
                eng.tensor_copy(iotab[:, :], iota_i[:, :]).then_inc(c_sem, 1)
                eng.tensor_copy(identb[:, :], ident[:, :]).then_inc(c_sem, 1)
                eng.memset(zerob[:, :], 0.0).then_inc(c_sem, 1)
                eng.memset(newM[:, :, :, :], -BIG).then_inc(c_sem, 1)
                eng.tensor_copy(sidx[:, 0, :], sidx_i[:, :]).then_inc(c_sem, 1)
                eng.tensor_copy(row[2][:, 0:T], rowi[2][:, 0:T]).then_inc(c_sem, 1)
                eng.wait_ge(load_sem, 16 * n_loads)
                for k in range(4):
                    eng.tensor_scalar(adiag[:, k, :], hmask[:, :], acol[:, k:k + 1], None, ALU.mult)\
                       .then_inc(c_sem, 1)

        shift, qshift = P.bit_length() - 1, Q.bit_length() - 1
        assert P == 1 << shift and Q == 1 << qshift
        e_rows = dst_pad.rearrange("(t e) -> t e", e=P)
        s_rows = src_pad.rearrange("(t e) -> t e", e=P)
        st_ = []
        ones_row = sb("ones_row", [1, P])

        def add(who, fn, n=1):
            st_.append((who, fn, n))

        def vec(fn, n=1):
            add("vector", lambda e, i: fn(e), n)

        def edge_column(e, k):
            of = e_rows[0:T, 0:1] if k == 0 else e_rows[0:T, P - 1:P]
            return e.dma_start(rowi[k][:, 0:T], of.rearrange("t o -> o t"), allow_slow_non_contiguous=True)

        def spread(of, n):
            def _(e, i):
                for a in range(0, n, 512):
                    z = min(n, a + 512)
                    ins = e.matmul(vall[:, a:z], ones_row[0:1, :], of[:, a:z], start=True, stop=True)
                return ins
            add("tensor", _)

        add("sync_dma", lambda e, i: [edge_column(e, 0), edge_column(e, 1)], 2)
        vec(lambda e: e.memset(ones_row[:, :], 1.0))
        vec(lambda e: [e.tensor_copy(row[0][:, 0:T], rowi[0][:, 0:T]), e.tensor_copy(row[1][:, 0:T], rowi[1][:, 0:T])], 2)
        for k in range(2):
            spread(row[k], T)
            vec(lambda e, k=k: e.tensor_copy(edges_all[k], vall[:, 0:T]))

        def fetch(k, c_):
            def _(e, i):
                return [e.indirect_dma_start(out=rows[n][:, c, :].bitcast(I32), out_offset=None, in_=of,
                                             in_offset=bass.IndirectOffsetOnAxis(ap=tb_i[:, 0, c:c + 1], axis=0))
                        for c in range(c_) for n, of in enumerate((e_rows, s_rows))]
            add("pool_dma", _, 2 * c_)

        def turn(of, c_, to):
            def _(e, i):
                for c in range(c_):
                    ins = e.transpose(psN[:, c, :], of[:, c, :], ident[:, :])
                return ins
            add("tensor", _)
            vec(lambda e: e.tensor_copy(to[:, :], psN[:, 0:c_, :].rearrange("p c s -> p (c s)")))

        def tables_of_steps(k, c_):
            dst_f, src_f = rows[2][:, 0:c_, :], rows[3][:, 0:c_, :]
            vec(lambda e: e.tensor_scalar(sidx[:, 3, :], sidx[:, 2, :], float(P), None, ALU.mult))
            vec(lambda e: e.tensor_copy(tb_i[:, :, :], sidx[:, 1:3, :]))
            add("sync_dma", lambda e, i: e.dma_start(block_drams[k].rearrange("(c p) -> p c", p=P), tb_i[:, 1, 0:c_],
                                                     allow_slow_non_contiguous=True))
            fetch(k, c_)
            vec(lambda e: [e.tensor_copy(dst_f, rows[0][:, 0:c_, :].bitcast(I32)),
                           e.tensor_copy(src_f, rows[1][:, 0:c_, :].bitcast(I32))], 2)
            if k:
                last_r, first_r = rows[4][:, 0:c_, :], rows[5][:, 0:c_, :]
                vec(lambda e: [e.memset(last_r[:, :, P - 1:P], 1.0), e.memset(first_r[:, :, 0:1], -BIG),
                               e.tensor_tensor(last_r[:, :, 0:P - 1], dst_f[:, :, 0:P - 1], dst_f[:, :, 1:P],
                                               ALU.not_equal)], 3)
                vec(lambda e: e.tensor_scalar(first_r[:, :, 1:P], last_r[:, :, 0:P - 1], -BIG, None, ALU.mult))
                for h, fd in first_drams.items():
                    add("sync_dma", lambda e, i, h=h, fd=fd: [
                        e.dma_start(fd.rearrange("(c s h) e -> s h c e", s=P, h=h)[:, n], first_r)
                        for n in range(h)], h)
                turn(last_r, c_, lastT)
            vec(lambda e: e.tensor_tensor(dst_f, dst_f, sidx[:, 3, 0:c_].unsqueeze(2).to_broadcast([P, c_, P]),
                                          ALU.subtract))
            turn(src_f, c_, srcT[k])
            turn(dst_f, c_, slotT[k])

        vec(lambda e: e.tensor_scalar(rowi[2][:, 0:T], rowi[0][:, 0:T], shift, None, ALU.logical_shift_right))
        vec(lambda e: e.tensor_copy(row[0][:, 0:T], rowi[2][:, 0:T]))
        vec(lambda e: e.tensor_tensor(row[0][:, 0:T], row[0][:, 0:T], row[2][:, 0:T], ALU.add))
        spread(row[0], T)
        vec(lambda e: e.tensor_copy(vsb[0][:, 0:T], vall[:, 0:T]))
        for c in range(SC):
            vec(lambda e, c=c: e.tensor_scalar(vsb[1][:, 0:T], vsb[0][:, 0:T], sidx[:, 0, c:c + 1], None,
                                               ALU.is_le, ALU.add, accum_out=sidx[:, 4, c:c + 1]))
        vec(lambda e: e.memset(sidx[:, 1, :], 0.0))
        vec(lambda e: e.tensor_scalar(sidx[:, 1, 0:SC], sidx[:, 4, 0:SC], -1.0, None, ALU.add))
        vec(lambda e: e.tensor_tensor(sidx[:, 2, :], sidx[:, 0, :], sidx[:, 1, :], ALU.subtract))
        tables_of_steps(0, SC)
        add("sync_dma", lambda e, i: e.dma_start(blk[:, :], block_drams[0].rearrange("(a s) -> a s", a=1)))
        blk_g, rel_g = (t[:, :].rearrange("p (g j) -> p g j", j=G) for t in (blk, blk_rel))
        vec(lambda e: e.tensor_tensor(rel_g, blk_g, blk_g[:, :, 0:1].to_broadcast([1, SP_ // G, G]), ALU.subtract))

        vec(lambda e: e.tensor_scalar(bcol[:, 0:1], sidx[:, 0, 0:1], float(P), None, ALU.mult))
        vec(lambda e: e.tensor_scalar(bcol[:, 1:2], bcol[:, 0:1], float(P), None, ALU.add))
        vec(lambda e: e.tensor_scalar(vsb[1][:, 0:T], edges_all[1], bcol[:, 0:1], None, ALU.is_lt, ALU.add,
                                      accum_out=bcol[:, 2:3]))
        vec(lambda e: e.tensor_scalar(vsb[1][:, 0:T], edges_all[0], bcol[:, 1:2], None, ALU.is_lt, ALU.add,
                                      accum_out=bcol[:, 3:4]))
        vec(lambda e: e.tensor_tensor(bcol[:, 4:5], bcol[:, 3:4], bcol[:, 2:3], ALU.subtract))
        vec(lambda e: e.tensor_scalar(bcol[:, 4:5], bcol[:, 4:5], 0.0, float(Q - 1), ALU.max, ALU.add))
        vec(lambda e: e.tensor_copy(bcol_i[:, :], bcol[:, 4:5]))
        vec(lambda e: e.tensor_scalar(bcol_i[:, :], bcol_i[:, :], qshift, None, ALU.logical_shift_right))
        vec(lambda e: e.tensor_copy(bcol[:, 5:6], bcol_i[:, :]))

        def block_rows(e, i):
            e.matmul(vall[:, 0:NB], bcol[:, 5:6].to_broadcast([P, P]), tri[:, :], start=True, stop=True)
            return e.matmul(vall[:, NB:2 * NB], bcol[:, 2:3].to_broadcast([P, P]), ident[:, 0:NB], start=True, stop=True)
        add("tensor", block_rows)
        vec(lambda e: e.tensor_scalar(brow[:, 0, :], vall[:, 0:NB], float(Q), None, ALU.mult))
        vec(lambda e: e.tensor_copy(brow[:, 1, :], vall[:, NB:2 * NB]))

        def by_step(ap):
            return ap.unsqueeze(2).to_broadcast([P, SCQ, NB])

        def by_block(ap):
            return ap.unsqueeze(1).to_broadcast([P, SCQ, NB])
        vec(lambda e: e.tensor_tensor(bwork[:, 0], by_block(brow[:, 0, :]), by_step(sidx[:, 0, :]), ALU.is_le))
        vec(lambda e: e.tensor_reduce(sidx[:, 2, :], bwork[:, 0], AX.X, ALU.add))
        vec(lambda e: e.tensor_scalar(sidx[:, 2, :], sidx[:, 2, :], -1.0, None, ALU.add))
        vec(lambda e: e.tensor_tensor(bwork[:, 0], by_block(iota[:, 0:NB]), by_step(sidx[:, 2, :]), ALU.is_equal))
        for k in range(2):
            vec(lambda e, k=k: e.tensor_tensor(bwork[:, 1], bwork[:, 0], by_block(brow[:, k, :]), ALU.mult))
            vec(lambda e, k=k: e.tensor_reduce(sidx[:, 4 + k, :], bwork[:, 1], AX.X, ALU.add))
        vec(lambda e: e.tensor_tensor(sidx[:, 1, :], sidx[:, 0, :], sidx[:, 4, :], ALU.subtract))
        vec(lambda e: e.tensor_tensor(sidx[:, 1, :], sidx[:, 1, :], sidx[:, 5, :], ALU.add))
        vec(lambda e: e.tensor_scalar(sidx[:, 1, :], sidx[:, 1, :], float(T), None, ALU.min))
        tables_of_steps(1, SCQ)
        NQ = SCQ * P // Q
        add("sync_dma", lambda e, i: e.dma_start(
            blkq[:, :], block_drams[1].rearrange("(q j) -> q j", j=Q)[:, 0:1].rearrange("q o -> o q"),
            allow_slow_non_contiguous=True))
        vec(lambda e: e.tensor_copy(row[0][:, 0:NQ], blkq[:, :]))
        vec(lambda e: [e.memset(row[1][:, 0:1], 1.0),
                       e.tensor_tensor(row[1][:, 1:NQ], row[0][:, 1:NQ], row[0][:, 0:NQ - 1], ALU.not_equal)], 2)
        spread(row[1], NQ)
        vec(lambda e: e.tensor_scalar(fresh[:, :], vall[:, 0:NQ], -BIG, None, ALU.mult))

        WT0, WTE, WTN = wbuf[:, 0, 0:D], wbuf[:, 0, D:3 * D], wbuf[:, 0, 3 * D:4 * D]
        WG = [wbuf[:, 1, 0:D + 2 * HEADS1], wbuf[:, 1, 2 * D:3 * D + 2 * HEADS1]]
        WX = wbuf[:, 2, :]
        w1t, w2t = acc[:, 0, 0:D], acc[:, 1, 0:D]

        def turn_w(e, i):
            for k, slot in enumerate((W0, WEA, WEB, WN, W1R, W2R)):
                ins = e.transpose(psN[:, k, :], wraw[:, slot, :], ident[:, :])
            return ins
        add("tensor", turn_w)
        add("vector", lambda e, i: e.tensor_copy(wbuf[:, 0, :].rearrange("p (k f) -> p k f", f=D), psN[:, 0:4, :]))
        add("vector", lambda e, i: e.tensor_copy(acc[:, 0:2, 0:D], psN[:, 4:6, :]))

        def w_by_a(e, i):
            for k, wt in enumerate((w1t, w2t)):
                ins = e.matmul(psS[:, 64 * k:64 * k + 2 * HEADS1], wt,
                               adiag[:, 2 * k:2 * k + 2, :].rearrange("p a h -> p (a h)"), start=True, stop=True)
            return ins
        add("tensor", w_by_a)
        for k, slot in enumerate((W1R, W2R)):
            add("vector", lambda e, i, k=k: e.tensor_copy(WG[k][:, D:D + 2 * HEADS1], psS[:, 64 * k:64 * k + 2 * HEADS1]))
            add("vector", lambda e, i, k=k, slot=slot: e.tensor_copy(WG[k][:, 0:D], wraw[:, slot, :]))
        for k, slot in enumerate((WKR, WVR, WQR, WSR)):
            add("vector", lambda e, i, k=k, slot=slot: e.tensor_copy(WX[:, k * D:(k + 1) * D], wraw[:, slot, :]))
        add("vector", lambda e, i: e.memset(acc[:, :, :], 0.0))
        add("vector", lambda e, i: e.memset(GT[:, :, :, D:D + 1], 1.0))
        chain(st_)

        DH = D + HEADS1
        R2 = V[:, 0, :, 0:D]

        def at(t, i):
            return t[:, bass.ds(i * G, G), :]

        def const(k, n):
            return consts[:, k:k + 1, :].to_broadcast([P, G, n])

        def wide(ap, n):
            return ap.unsqueeze(len(ap.shape)).to_broadcast([*ap.shape, n])

        def heads(ap, h):
            return ap.rearrange("p g (h c) -> p g h c", h=h)

        def node_phase(stages, table=None, rows_of=None):
            if table is not None:
                stages = stages + [("sync_dma", lambda e, i: e.dma_start(
                    at(table.rearrange("(b p) f -> p b f", p=P), i), rows_of[:, :, 0:table.shape[1]]))]
            chain(stages, NBAT)

        def norm_stages():
            mean, var, dev = st[:, 0, 0:G], st[:, 1, 0:G], st[:, 2, 0:G]
            return [
                ("vector", lambda e, i: e.tensor_reduce(mean, at(X, i), AX.X, ALU.add)),
                ("vector", lambda e, i: e.tensor_scalar(mean, mean, 1.0 / D, None, ALU.mult)),
                ("vector", lambda e, i: e.tensor_tensor(Y[:, :, :], at(X, i), wide(mean, D), ALU.subtract)),
                ("scalar", lambda e, i: e.activation(Y2[:, :, :], Y[:, :, :], ACT.Square)),
                ("vector", lambda e, i: e.tensor_reduce(var, Y2[:, :, :], AX.X, ALU.add)),
                ("vector", lambda e, i: e.tensor_scalar(var, var, 1.0 / D, LN_EPS, ALU.mult, ALU.add)),
                ("scalar", lambda e, i: e.activation(dev, var, ACT.Sqrt)),
                ("vector", lambda e, i: e.reciprocal(var, dev)),
                ("vector", lambda e, i: e.scalar_tensor_tensor(
                    out=Y[:, :, :], in0=Y[:, :, :], scalar=0.0, in1=wide(var, D), op0=ALU.max, op1=ALU.mult)),
            ]

        def turn_stages():
            def turn_y(e, i):
                for g in range(G):
                    ins = e.transpose(psN[:, g, :], Y[:, g, :], ident[:, :])
                return ins
            return [("tensor", turn_y), ("scalar", lambda e, i: e.copy(YT[:, :, :], psN[:, :, :]))]

        def product(w):
            def mm(e, i):
                for g in range(G):
                    ins = e.matmul(psD[:, g, 0:w.shape[1]], YT[:, g, :], w, start=True, stop=True)
                return ins
            return ("tensor", mm)

        def plus_bias(to, k):
            return ("vector", lambda e, i: e.tensor_tensor(
                to(i), psD[:, :, :], bias[:, k:k + 1, :].to_broadcast([P, G, D]), ALU.add))

        def split_stages(of, to):
            w = to(0).shape[-1]
            rest = R2[:, :, 0:w]
            return [
                ("scalar", lambda e, i: e.copy(to(i)[:, :, 0, :], top(of))),
                ("vector", lambda e, i: e.tensor_tensor(rest, of, top(of), ALU.subtract)),
                ("scalar", lambda e, i: e.copy(to(i)[:, :, 1, :], top(rest))),
                ("vector", lambda e, i: e.tensor_tensor(to(i)[:, :, 2, :], rest, top(rest), ALU.subtract)),
            ]

        def x_plus(y):
            return ("vector", lambda e, i: e.tensor_tensor(at(X, i), at(X, i), y, ALU.add))

        def clear_acc():
            return ("vector", lambda e, i: e.tensor_copy(at(acc, i), const(0, DH)))

        def mean_stages(w, k, relu):
            out_ = [
                ("vector", lambda e, i: e.tensor_tensor(Y[:, :, :], at(acc, i)[:, :, 0:D], wide(st[:, 0, 0:G], D), ALU.mult)),
                clear_acc(), *turn_stages(), product(w), plus_bias(lambda i: Y[:, :, :], k),
            ]
            if relu:
                return out_ + [("vector", lambda e, i: e.scalar_tensor_tensor(
                    out=at(X, i), in0=Y[:, :, :], scalar=0.0, in1=at(X, i), op0=ALU.max, op1=ALU.add))]
            return out_ + [x_plus(Y[:, :, :])]

        def softmax_stages(h, op, eps):
            sums = lambda i: at(acc, i)[:, :, 0:D + h].rearrange("p g (h c) -> p g h c", h=h)
            c = D // h
            den = st[:, 0, 0:G * h].rearrange("p (g h) -> p g h", h=h)
            den4 = den.unsqueeze(3)
            return [
                ("vector", lambda e, i: e.tensor_scalar(den4, sums(i)[:, :, :, c:c + 1], eps, None, op)),
                ("vector", lambda e, i: e.reciprocal(den, den)),
                ("vector", lambda e, i: e.tensor_tensor(heads(Y[:, :, :], h), sums(i)[:, :, :, 0:c], wide(den, c), ALU.mult)),
            ]

        def gat_stages(wg):
            d0 = D + HEADS1
            s4 = lambda i: at(acc, i).rearrange("p g (h c) -> p g h c", h=HEADS1)
            c = D // HEADS1
            return [
                product(wg[:, 0:D]),
                ("scalar", lambda e, i: e.copy(R[:, :, 0:D], psD[:, :, :])),
                product(wg[:, D:D + 2 * HEADS1]),
                ("vector", lambda e, i: e.tensor_copy(R[:, :, D:d0], psD[:, :, 0:HEADS1])),
                ("vector", lambda e, i: e.tensor_copy(Y2[:, :, HEADS1:2 * HEADS1], psD[:, :, HEADS1:2 * HEADS1])),
                ("vector", lambda e, i: e.tensor_tensor(Y2[:, :, 0:HEADS1], R[:, :, D:d0], Y2[:, :, HEADS1:2 * HEADS1], ALU.add)),
                *split_stages(Y2[:, :, HEADS1:2 * HEADS1], lambda i: at(nodeD, i)),
                ("vector", lambda e, i: e.scalar_tensor_tensor(
                    out=at(nodeM, i), in0=Y2[:, :, 0:HEADS1], scalar=0.2, in1=Y2[:, :, 0:HEADS1],
                    op0=ALU.mult, op1=ALU.max)),
                ("vector", lambda e, i: e.tensor_copy(at(acc, i), const(1, DH))),
                ("vector", lambda e, i: e.tensor_copy(s4(i)[:, :, :, 0:c], heads(R[:, :, 0:D], HEADS1))),
            ]

        signals = {}
        names = ("index", "staged", "onehot", "onehot32", "turned", "onehotT", "toedge", "prod", "head", "logit",
                 "logitT", "seg", "segT", "nmax", "pen", "tmax", "qmax", "drop", "resc", "lastmax1", "lastmax2", "newM1", "newM2", "maxedge", "below", "bound",
                 "weight", "values", "sums", "added")
        for n in names:
            signals[n] = Signal(sem(n))
        for n, per in (("lastmax", 2), ("mmax", 2 * QS), ("qscaled", QS), ("qadded", QS)):
            signals[n] = Signal(sem(n), per)
        ring_rows = [Signal(sem(f"rows{r}"), 1, 16 * G) for r in range(RING)]
        ring_first = [Signal(sem(f"first{r}"), 1, 16) for r in range(RING)]
        with nc.Block() as block:
            @block.gpsimd
            def _(eng):
                for sg in signals.values():
                    sg.base = RING * sg.per
                    eng.sem_inc(sg.sem, sg.base)

        def wait(name, eng, g, k=None):
            signals[name].wait(eng, g, k)

        used = set()

        def done(name, ins):
            used.add(name)
            signals[name].done(ins)

        def at_block(t, b, w):
            return t[:, bass.ds(b, 1), 0:w].rearrange("p o w -> p (o w)")

        def at_part(t, b, part):
            return t[:, bass.ds(b, 1), part, :].rearrange("p o w -> p (o w)")

        def table_ready(eng):
            eng.wait_ge(chain_sems["sync_dma"].sem, chain_sems["sync_dma"].base)

        reg_sets = {}

        def loaded(eng, which, table, g, n, most):
            if (eng.engine, which) not in reg_sets:
                reg_sets[eng.engine, which] = [eng.alloc_register(f"{which}_{j}") for j in range(n)]
            regs = reg_sets[eng.engine, which]
            eng.load(regs, table[0:1, bass.ds(g * n, n)])
            return [eng.snap(r, min_val=0, max_val=most) for r in regs]

        def over_groups(eng, n, turn, ahead=0):
            last = (n - ahead) // RING
            for k in range(RING):
                turn(0, k, k)
            with eng.Fori(1, last) as i:
                for k in range(RING):
                    turn(i, k, i * RING + k)
            for g in range(last * RING, n):
                turn(g // RING, g % RING, g)

        def next_of(i, k, n=1):
            return (i, k + n) if k + n < RING else (i + 1, k + n - RING)

        def previous(i, k, n=1):
            return (i, k - n) if k >= n else (i - 1, k - n + RING)

        def there(g, n):
            return not isinstance(g, int) or g < n

        def fetch_rows(eng, table, k, g, release):
            wait(release, eng, g - RING)
            wait("index", eng, g)
            table_ready(eng)
            apart(eng)
            for j in range(G):
                eng.indirect_dma_start(
                    out=GT[:, k, j, 0:table.shape[1]], out_offset=None, in_=table,
                    in_offset=bass.IndirectOffsetOnAxis(ap=srcI[:, k, j:j + 1], axis=0),
                ).then_inc(ring_rows[k].sem, 16)

        def copy_index(eng, steps, i, k, g):
            if not (isinstance(i, int) and i == 0):
                ring_rows[k].wait(eng, i - 1)
            done("index", eng.copy(srcI[:, k, :], srcT[steps][:, bass.ds(g * G, G)]))

        def one_hot(eng, out_, steps, g):
            return eng.tensor_tensor(out_, iotab[:, :].unsqueeze(1).to_broadcast([P, G, P]),
                                     wide(slotT[steps][:, bass.ds(g * G, G)], P), ALU.is_equal)

        def run_pass(n, parts, pool_release, table, sync=None):
            ahead = {"AA": 2, "A": 1, "B": 0, "C": -1, "CC": -2, "I": RING}

            def run(eng, own):
                look = max(ahead[what] for what, _ in own)
                for what, fn in sorted(own, key=lambda part: -ahead[part[0]]):
                    for g in range(ahead[what]):
                        fn(eng, g // RING, g % RING, g)

                def turn(i, k, g):
                    for what, fn in own:
                        n_ = ahead[what]
                        if n_ < 0:
                            if isinstance(g, int) and g + n_ < 0:
                                continue
                            ii, kk = previous(i, k, -n_)
                        elif n_ == RING:
                            ii, kk = i + 1, k
                        else:
                            ii, kk = next_of(i, k, n_)
                        if there(g + n_, n):
                            fn(eng, ii, kk, g + n_)
                over_groups(eng, n, turn, look)
                for end in range(n, n + 2):
                    for what, fn in own:
                        g = end + ahead[what]
                        if g < n:
                            fn(eng, g // RING, g % RING, g)

            with nc.Block() as block:
                @block.gpsimd
                def _(eng):
                    over_groups(eng, n, lambda i, k, g: fetch_rows(eng, table, k, g, pool_release))

                @block.sync
                def _(eng):
                    if sync:
                        over_groups(eng, n, lambda i, k, g: sync(eng, i, k, g))

                @block.scalar
                def _(eng):
                    run(eng, parts["scalar"])

                @block.tensor
                def _(eng):
                    run(eng, parts["tensor"])

                @block.vector
                def _(eng):
                    table_ready(eng)
                    run(eng, parts["vector"])

            for name in used:
                signals[name].close(n)
            used.clear()
            for k in range(RING):
                for r in (ring_rows, ring_first) if sync else (ring_rows,):
                    r[k].close(-(-(n - k) // RING))

        def sum_pass(kind, table):
            mlp = kind == "mlp"
            VW = D if mlp else D + 1
            dve_b = {}

            def act_A(eng, i, k, g):
                q = k % 2
                wait("onehot", eng, g)
                wait("sums", eng, g - 2)
                done("onehot32", eng.copy(O[:, q, :, :], Ob[:, q, :, :]))
                wait("turned", eng, g)
                wait("toedge", eng, g - 2)
                done("onehotT", eng.copy(Ot[:, q, :, :], psT[:, :, :]))

            def act_relu(eng, i, k, g):
                wait("prod", eng, g)
                wait("sums", eng, g - 2)
                done("values", eng.activation(V[:, k % 2, :, 0:D], prod[:, :, :], ACT.Relu))

            def pe_A(eng, i, k, g):
                q = k % 2
                wait("onehot", eng, g)
                wait("onehotT", eng, g - 1)
                for j in range(G):
                    ins = eng.transpose(psT[:, j, :], Ob[:, q, j, :], identb[:, :])
                done("turned", ins)
                b = loaded(eng, "blocks", blk, g, G, NB - 1)
                wait("onehotT", eng, g)
                wait("prod", eng, g - 1)
                for j in range(G):
                    for part in range(3):
                        ins = eng.matmul(psD[:, j, :], Ot[:, q, j, :], at_part(nodeQ, b[j], part), start=part == 0,
                                         stop=part == 2)
                done("toedge", ins)

            def pe_B(eng, i, k, g):
                q = k % 2
                if mlp:
                    wait("values", eng, g)
                else:
                    ring_rows[k].wait(eng, i)
                wait("onehot32", eng, g)
                wait("added", eng, g - 1)
                place = loaded(eng, "places", blk_rel, g, G, G - 1)
                for n in range(0, G, 2):
                    eng.matmul(psA[:, n:n + 2, 0:VW], zerob[0:1, 0:P], zerob[0:1, 0:2 * VW], start=True, stop=False,
                               skip_group_check=True)
                for j in range(G):
                    val = V[:, q, j, 0:VW] if mlp else GT[:, k, j, 0:VW]
                    to = psA[:, bass.ds(place[j], 1), 0:VW].rearrange("p o w -> p (o w)")
                    ins = eng.matmul(to, O[:, q, j, :], val, start=False, stop=j == G - 1, skip_group_check=True)
                done("sums", ins)

            def dve_A(eng, i, k, g):
                if mlp:
                    wait("turned", eng, g - 2)
                    wait("onehot32", eng, g - 2)
                    done("onehot", one_hot(eng, Ob[:, k % 2, :, :], 0, g))
                else:
                    wait("sums", eng, g - 2)
                    done("onehot32", one_hot(eng, O[:, k % 2, :, :], 0, g))

            def dve_prod(eng, i, k, g):
                ring_rows[k].wait(eng, i)
                wait("toedge", eng, g)
                wait("values", eng, g - 1)
                done("prod", eng.tensor_tensor(prod[:, :, :], psD[:, :, :], GT[:, k, :, 0:D], ALU.add))

            def dve_C(eng, i, k, g):
                b = loaded(eng, "blocks", blk, g, G, NB - 1)
                a = acc[:, bass.ds(b[0], G), 0:VW]
                wait("sums", eng, g)
                wait("added", eng, g - 1)
                done("added", eng.tensor_tensor(a, a, psA[:, :, 0:VW], ALU.add))

            index = ("I", lambda eng, i, k, g: copy_index(eng, 0, i, k, g))
            run_pass(NG, {
                "scalar": (("A", act_A), index, ("A", act_relu)) if mlp else (index,),
                "tensor": (("A", pe_A), ("B", pe_B)) if mlp else (("B", pe_B),),
                "vector": (("A", dve_A), ("C", dve_C), ("A", dve_prod)) if mlp else (("A", dve_A), ("C", dve_C)),
            }, "prod" if mlp else "sums", table)

        srcI = sb("srcI", [P, RING, G], I32)
        quantD = sb("quantD", [P, 2, QS, 3, D], BF16)
        quantZ = sb("quantZ", [P, 2, QS, HEADS1])
        quantF = sb("quantF", [P, 2, QS])

        def softmax_pass(kind, table, h):
            gat = kind == "gat"
            HG, C = h * G, D // h
            VW = D + h
            f0 = 0 if gat else D
            dw = h if gat else D
            flatA = psA[:, :, :].rearrange("p g w -> p (g w)")
            assert 4 * QS * 256 <= 1024 * 2
            logT, segR = flatA[0:HG, 1024:1024 + P], flatA[:, 1024 + P:1024 + P + HG]
            maxima = psS[:, 0:G * (h + 1)].rearrange("p (g w) -> p g w", g=G)
            edge_max = psS[:, 256:256 + HG].rearrange("p (g h) -> p g h", g=G)

            def by_head(ap):
                return ap.rearrange("p (g h) -> p g h", g=G)

            def first_rows(eng, i, k, g):
                wait("seg", eng, g - RING)
                ring_first[k].done(eng.dma_start(first[0:HG, k, :], first_drams[h][bass.ds(g * HG, HG), :]))

            def stage(eng, i, k, g):
                q = k % 2
                b = loaded(eng, f"quanta{q}", blkq, g, QS, NB - 1)
                wait("toedge", eng, g - 2)
                wait("mmax", eng, g - 2)
                for u in range(QS):
                    eng.copy(quantD[:, q, u, :, 0:dw], (nodeD if gat else nodeQ)[:, bass.ds(b[u], 1), :, :]
                             .rearrange("p o k w -> p (o k) w"))
                    eng.copy(quantZ[:, q, u, 0:h], at_block(nodeM, b[u], h))
                done("staged", eng.copy(quantF[:, q, :], fresh[:, bass.ds(g * QS, QS)]))

            def act_turned(eng, i, k, g):
                wait("turned", eng, g)
                wait("maxedge", eng, g - RING)
                done("onehotT", eng.copy(Ot[:, k, :, :], psT[:, :, :]))

            def act_onehot32(eng, i, k, g):
                wait("onehot", eng, g)
                wait("sums", eng, g - 2)
                done("onehot32", eng.copy(O[:, k % 2, :, :], Ob[:, k, :, :]))

            def act_resc(eng, i, k, g):
                q = k % 2
                wait("drop", eng, g)
                wait("qadded", eng, g - 2)
                done("resc", eng.activation(resc[:, q, 0:QS, 0:h], diff[:, q, 0:QS, 0:h], ACT.Exp))

            def act_weight(eng, i, k, g):
                q = k % 2
                wait("bound", eng, g)
                wait("sums", eng, g - 2)
                v = V[:, q, :, 0:VW].rearrange("p g (h c) -> p g h c", h=h)
                done("weight", eng.activation(v[:, :, :, C:C + 1], by_head(below[:, q, 0:HG]).unsqueeze(3), ACT.Exp))

            def pe_turn(eng, i, k, g):
                wait("onehot", eng, g)
                wait("onehotT", eng, g - 1)
                for j in range(G):
                    ins = eng.transpose(psT[:, j, :], Ob[:, k, j, :], identb[:, :])
                done("turned", ins)

            def pe_toedge(eng, i, k, g):
                q = k % 2
                wait("staged", eng, g)
                wait("onehotT", eng, g)
                wait("prod", eng, g - 1)
                for j in range(G):
                    for part in range(3):
                        ins = eng.matmul(psD[:, j, 0:dw], Ot[:, k, j, :], quantD[:, q, j // Q, part, 0:dw],
                                         start=part == 0, stop=part == 2)
                done("toedge", ins)

            def pe_logitT(eng, i, k, g):
                wait("logit", eng, g)
                wait("lastmax", eng, g - 1)
                done("logitT", eng.transpose(logT, lg[:, k % 2, 0:HG], ident[:, :]))

            def pe_segT(eng, i, k, g):
                wait("seg", eng, g)
                if HG < P:
                    apart(eng)
                done("segT", eng.transpose(segR, seg[0:HG, k % 2, :], ident[0:HG, 0:HG]))

            def pe_maxima(eng, i, k, g):
                q = k % 2
                wait("onehot", eng, g)
                wait("lastmax2", eng, g)
                wait("below", eng, g - 1)
                for j in range(G):
                    for n, part in enumerate((top(lastmax[:, q, j, 0:h + 1]), top(lastmax1[:, q, j, 0:h + 1]),
                                              lastmax2[:, q, j, 0:h + 1])):
                        ins = eng.matmul(maxima[:, j, :], Ob[:, k, j, :], part, start=n == 0, stop=n == 2)
                done("nmax", ins)

            def pe_maxedge(eng, i, k, g):
                q = k % 2
                wait("newM2", eng, g)
                for j in range(G):
                    u = j // Q
                    for n, part in enumerate((top(newM[:, q, u, 0:h]), top(newM1[:, q, u, 0:h]), newM2[:, q, u, 0:h])):
                        ins = eng.matmul(edge_max[:, j, :], Ot[:, k, j, :], part, start=n == 0, stop=n == 2)
                done("maxedge", ins)

            def pe_sums(eng, i, k, g):
                q = k % 2
                wait("values", eng, g)
                wait("onehot32", eng, g)
                wait("qadded", eng, g - 2)
                for j in range(G):
                    ins = eng.matmul(psA[:, q * QS + j // Q, 0:VW], O[:, q, j, :], V[:, q, j, 0:VW],
                                     start=j % Q == 0, stop=j % Q == Q - 1)
                done("sums", ins)

            def dve_onehot(eng, i, k, g):
                wait("nmax", eng, g - RING)
                wait("turned", eng, g - RING)
                wait("onehot32", eng, g - RING)
                done("onehot", one_hot(eng, Ob[:, k, :, :], 1, g))

            def dve_prod(eng, i, k, g):
                ring_rows[k].wait(eng, i)
                wait("toedge", eng, g)
                if gat:
                    done("prod", eng.tensor_tensor(by_head(lg2[:, 0:HG]), psD[:, :, 0:h], GT[:, k, :, D:D + h], ALU.add))
                else:
                    done("prod", eng.tensor_tensor(prod[:, :, :], psD[:, :, :], GT[:, k, :, 0:D], ALU.mult))

            def dve_logit(eng, i, k, g):
                q = k % 2
                wait("prod", eng, g)
                wait("below", eng, g - 2)
                if gat:
                    done("logit", eng.scalar_tensor_tensor(
                        out=lg[:, q, 0:HG], in0=lg2[:, 0:HG], scalar=0.2, in1=lg2[:, 0:HG],
                        op0=ALU.mult, op1=ALU.max))
                else:
                    done("logit", eng.tensor_reduce(
                        lg[:, q, 0:HG], prod[:, :, :].rearrange("p g (h c) -> p (g h) c", h=h), AX.X, ALU.add))

            def dve_seg(eng, i, k, g):
                wait("logitT", eng, g)
                ring_first[k].wait(eng, i)
                wait("segT", eng, g - 2)
                done("seg", eng.tensor_tensor_scan(seg[0:HG, k % 2, :], first[0:HG, k, :], logT, -BIG, ALU.add, ALU.max))

            def dve_lastmax(eng, i, k, g):
                q = k % 2
                wait("segT", eng, g)
                wait("nmax", eng, g - 2)
                last = lastT[:, bass.ds(g * G, G)]
                done("lastmax", eng.tensor_tensor(lastmax[:, q, :, 0:h], by_head(segR), wide(last, h), ALU.mult))
                done("lastmax", eng.tensor_copy(lastmax[:, q, :, h:h + 1], last.unsqueeze(2)))
                of, rest = lastmax[:, q, :, 0:h + 1], lastmax1[:, q, :, 0:h + 1]
                wait("lastmax", eng, g)
                done("lastmax1", eng.tensor_tensor(rest, of, top(of), ALU.subtract))
                wait("lastmax1", eng, g)
                done("lastmax2", eng.tensor_tensor(lastmax2[:, q, :, 0:h + 1], rest, top(rest), ALU.subtract))

            def before(eng, i, k, g, u):
                q = k % 2
                if u:
                    wait("mmax", eng, g, 2 * u - 1)
                else:
                    wait("staged", eng, g)
                    wait("drop", eng, g - 2)
                    wait("mmax", eng, g - 1)
                last = newM[:, q, u - 1, 0:h] if u else newM[:, 1 - q, QS - 1, 0:h]
                done("mmax", eng.scalar_tensor_tensor(
                    out=oldM[:, q, u, 0:h], in0=last, scalar=quantF[:, q, u:u + 1], in1=quantZ[:, q, u, 0:h],
                    op0=ALU.add, op1=ALU.max))

            def after(eng, i, k, g, u):
                q = k % 2
                wait("mmax", eng, g, 2 * u)
                if not u:
                    wait("maxedge", eng, g - 2)
                    wait("qmax", eng, g)
                done("mmax", eng.tensor_tensor(newM[:, q, u, 0:h], oldM[:, q, u, 0:h], qmax[:, q, u, 0:h], ALU.max))

            def dve_before(eng, i, k, g):
                before(eng, i, k, g, 0)

            def dve_pen(eng, i, k, g):
                wait("nmax", eng, g)
                done("pen", eng.tensor_scalar(pen[:, k % 2, :].unsqueeze(2), maxima[:, :, h:h + 1], BIG, -BIG,
                                              ALU.mult, ALU.add))

            def dve_tmax(eng, i, k, g):
                q = k % 2
                wait("pen", eng, g)
                done("tmax", eng.tensor_tensor(tmax[:, q, :, 0:h], maxima[:, :, 0:h], wide(pen[:, q, :], h), ALU.add))

            def dve_qmax(eng, i, k, g):
                q = k % 2
                wait("tmax", eng, g)
                done("qmax", eng.tensor_reduce(qmax[:, q, :, 0:h], tmax[:, q, :, 0:h].rearrange("p (u j) h -> p u h j", j=Q),
                                               AX.X, ALU.max))

            def dve_max(eng, i, k, g):
                q = k % 2
                after(eng, i, k, g, 0)
                for u in range(1, QS):
                    before(eng, i, k, g, u)
                    after(eng, i, k, g, u)
                wait("mmax", eng, g)
                of, rest = newM[:, q, :, 0:h], newM1[:, q, :, 0:h]
                done("newM1", eng.tensor_tensor(rest, of, top(of), ALU.subtract))
                wait("resc", eng, g - 2)
                done("drop", eng.tensor_tensor(diff[:, q, 0:QS, 0:h], oldM[:, q, 0:QS, 0:h], newM[:, q, :, 0:h],
                                               ALU.subtract))
                wait("newM1", eng, g)
                done("newM2", eng.tensor_tensor(newM2[:, q, :, 0:h], rest, top(rest), ALU.subtract))

            def dve_below(eng, i, k, g):
                q = k % 2
                wait("maxedge", eng, g)
                wait("weight", eng, g - 2)
                done("below", eng.tensor_tensor(by_head(below[:, q, 0:HG]), by_head(lg[:, q, 0:HG]), edge_max,
                                                ALU.subtract))
                wait("below", eng, g)
                done("bound", eng.tensor_scalar(below[:, q, 0:HG], below[:, q, 0:HG], 0.0, None, ALU.min))

            def dve_values(eng, i, k, g):
                wait("weight", eng, g)
                v = V[:, k % 2, :, 0:VW].rearrange("p g (h c) -> p g h c", h=h)
                done("values", eng.tensor_tensor(
                    v[:, :, :, 0:C], heads(GT[:, k, :, f0:f0 + D], h),
                    v[:, :, :, C:C + 1].to_broadcast([P, G, h, C]), ALU.mult))

            def scale_sums(eng, i, k, g, u):
                a = at_block(acc, blocks[u], VW).rearrange("p (h c) -> p h c", h=h)
                wait("resc", eng, g)
                wait("qadded", eng, g if u else g - 1, u - 1 if u else None)
                done("qscaled", eng.tensor_tensor(a, a, wide(resc[:, k % 2, u, 0:h], C + 1), ALU.mult))

            def add_sums(eng, i, k, g, u):
                a = at_block(acc, blocks[u], VW)
                wait("sums", eng, g)
                wait("qscaled", eng, g, u)
                done("qadded", eng.tensor_tensor(a, a, psA[:, k % 2 * QS + u, 0:VW], ALU.add))

            def dve_scale(eng, i, k, g):
                blocks[:] = loaded(eng, "quanta", blkq, g, QS, NB - 1)
                scale_sums(eng, i, k, g, 0)

            def dve_add(eng, i, k, g):
                add_sums(eng, i, k, g, 0)
                for u in range(1, QS):
                    scale_sums(eng, i, k, g, u)
                    add_sums(eng, i, k, g, u)

            blocks = []
            index = ("I", lambda eng, i, k, g: copy_index(eng, 1, i, k, g))
            run_pass(NGQ, {
                "scalar": (index, ("B", act_resc), ("AA", act_turned), ("B", act_weight), ("AA", stage),
                           ("B", act_onehot32)),
                "tensor": (("B", pe_maxima), ("A", pe_toedge), ("AA", pe_turn), ("A", pe_logitT), ("B", pe_maxedge),
                           ("A", pe_segT), ("C", pe_sums)),
                "vector": (("AA", dve_onehot), ("B", dve_before), ("B", dve_pen), ("A", dve_prod), ("B", dve_tmax),
                           ("A", dve_logit), ("B", dve_qmax), ("B", dve_max), ("CC", dve_scale), ("A", dve_seg),
                           ("CC", dve_add), ("B", dve_below), ("A", dve_lastmax), ("B", dve_values)),
            } if gat else {
                "scalar": (index, ("AA", act_turned), ("AA", stage), ("B", act_weight), ("B", act_resc),
                           ("B", act_onehot32)),
                "tensor": (("B", pe_maxima), ("AA", pe_turn), ("A", pe_logitT), ("B", pe_maxedge),
                           ("A", pe_segT), ("AA", pe_toedge), ("C", pe_sums)),
                "vector": (("AA", dve_onehot), ("A", dve_prod), ("A", dve_logit), ("B", dve_before), ("B", dve_pen),
                           ("B", dve_tmax), ("B", dve_qmax), ("B", dve_max), ("CC", dve_scale), ("A", dve_seg),
                           ("CC", dve_add), ("B", dve_below), ("A", dve_lastmax), ("B", dve_values)),
            }, "values", table, first_rows)

        T0, T1, T2, T3, T4 = tables
        node_phase(norm_stages(), T0, Y)
        sum_pass("sum", T0)

        recip = ("vector", lambda e, i: e.reciprocal(st[:, 0, 0:G], st[:, 1, 0:G]))
        node_phase([
            ("vector", lambda e, i: e.tensor_copy(at(deg, i), at(acc, i)[:, :, D:D + 1])),
            ("vector", lambda e, i: e.tensor_scalar(st[:, 1, 0:G].unsqueeze(2), at(deg, i), MEAN_EPS, None, ALU.add)),
            recip, *mean_stages(WT0, 0, False), *norm_stages(), *turn_stages(),
            product(WTE[:, 0:D]), ("scalar", lambda e, i: e.copy(R[:, :, 0:D], psD[:, :, :])),
            product(WTE[:, D:2 * D]), ("vector", lambda e, i: e.tensor_copy(Y2[:, :, :], psD[:, :, :])),
            *split_stages(Y2[:, :, :], lambda i: at(nodeQ, i)),
        ], T1, R)
        sum_pass("mlp", T1)

        node_phase([
            ("vector", lambda e, i: e.tensor_scalar(st[:, 1, 0:G].unsqueeze(2), at(deg, i), 1.0, None, ALU.max)),
            recip, *mean_stages(WTN, 1, True), *norm_stages(), *turn_stages(), *gat_stages(WG[0]),
        ], T2, R)
        softmax_pass("gat", T2, HEADS1)

        node_phase([
            *softmax_stages(HEADS1, ALU.add, SOFTMAX_EPS),
            ("vector", lambda e, i: e.tensor_tensor(Y[:, :, :], Y[:, :, :], bias[:, 2:3, :].to_broadcast([P, G, D]), ALU.add)),
            ("vector", lambda e, i: e.tensor_scalar(Y2[:, :, :], Y[:, :, :], 0.0, None, ALU.min)),
            ("scalar", lambda e, i: e.activation(Y2[:, :, :], Y2[:, :, :], ACT.Exp)),
            ("vector", lambda e, i: e.tensor_scalar(Y2[:, :, :], Y2[:, :, :], -1.0, None, ALU.add)),
            ("vector", lambda e, i: e.scalar_tensor_tensor(out=Y[:, :, :], in0=Y[:, :, :], scalar=0.0,
                                                           in1=Y2[:, :, :], op0=ALU.max, op1=ALU.add)),
            *turn_stages(), *gat_stages(WG[1]),
        ], T3, R)
        softmax_pass("gat", T3, HEADS1)

        node_phase([
            *softmax_stages(HEADS1, ALU.add, SOFTMAX_EPS),
            ("vector", lambda e, i: e.tensor_tensor(Y[:, :, :], Y[:, :, :], bias[:, 3:4, :].to_broadcast([P, G, D]), ALU.add)),
            x_plus(Y[:, :, :]), clear_acc(), ("vector", lambda e, i: e.tensor_copy(at(nodeM, i), const(2, HEADS1))),
            *norm_stages(), *turn_stages(),
            product(WX[:, 0:D]), plus_bias(lambda i: R[:, :, 0:D], 4),
            product(WX[:, D:2 * D]), plus_bias(lambda i: R[:, :, D:2 * D], 5),
            product(WX[:, 2 * D:3 * D]), plus_bias(lambda i: Y2[:, :, :], 6),
            ("vector", lambda e, i: e.tensor_scalar(Y2[:, :, :], Y2[:, :, :], float(D // HEADS3) ** -0.5, None, ALU.mult)),
            *split_stages(Y2[:, :, :], lambda i: at(nodeQ, i)),
            product(WX[:, 3 * D:4 * D]), plus_bias(lambda i: Y[:, :, :], 7), x_plus(Y[:, :, :]),
        ], T4, R)
        softmax_pass("dot", T4, HEADS3)

        node_phase([*softmax_stages(HEADS3, ALU.max, SOFTMAX_EPS), x_plus(Y[:, :, :])])
        chain([
            ("sync_dma", lambda e, i: e.dma_start(out[0:FULL * P, :].rearrange("(b p) f -> p b f", p=P), X[:, 0:FULL, :])),
            ("sync_dma", lambda e, i: e.dma_start(out[FULL * P:N, :], X[0:REST, FULL, :])),
        ])
        with nc.Block() as block:
            @block.sync
            def _(eng):
                table_ready(eng)


INPUTS = ["x", "src", "dst", "L0_gnn_W", "L0_gnn_b", "L1_gnn_W_edge", "L1_gnn_W_node", "L1_gnn_b_node",
          "L2_gnn_W1", "L2_gnn_a_src1", "L2_gnn_a_dst1", "L2_gnn_b1", "L2_gnn_W2", "L2_gnn_a_src2",
          "L2_gnn_a_dst2", "L2_gnn_b2", "L3_gnn_Wq", "L3_gnn_bq", "L3_gnn_Wk", "L3_gnn_bk", "L3_gnn_Wv",
          "L3_gnn_bv", "L3_gnn_Wskip", "L3_gnn_bskip"]


def kernel(**inputs):
    import numpy as np
    from concourse import bacc
    from concourse.bass_utils import run_bass_kernel_spmd

    nc = bacc.Bacc("TRN2", target_bir_lowering=False, num_devices=1)
    arrays, args = {}, []
    for name in INPUTS:
        a = np.ascontiguousarray(inputs[name])
        arrays[f"in_{name}"] = a
        args.append(nc.dram_tensor(f"in_{name}", a.shape, mybir.dt.from_np(a.dtype), kind="ExternalInput").ap())
    shape = inputs["x"].shape
    out = nc.dram_tensor("out", shape, F32, kind="ExternalOutput").ap()
    program(nc, *args, out)
    r = run_bass_kernel_spmd(nc, [arrays], core_ids=[0])
    return r.results[0]["out"]
```

```python
from contextlib import ExitStack

import concourse.bass as bass
from concourse import mybir

F32 = mybir.dt.float32
BF16 = mybir.dt.bfloat16
I32 = mybir.dt.int32
ALU = mybir.AluOpType
ACT = mybir.ActivationFunctionType
AX = mybir.AxisListType

P = 128
G = 8
Q = 4
RING = 4
BIG = 1.0e30
LN_EPS = 1e-5
MEAN_EPS = 1e-6
SOFTMAX_EPS = 1e-16


class Signal:

    def __init__(self, sem, per=1, by=1):
        self.sem, self.per, self.by, self.base = sem, per, by, 0

    def done(self, ins):
        ins.then_inc(self.sem, self.by)

    def value(self, rnd, k=None):
        k = self.per if k is None else k + 1
        return (rnd * self.per + k) * self.by + self.base

    def wait(self, eng, rnd, k=None):
        v = self.value(rnd, k)
        if not isinstance(v, int) or v > self.base:
            eng.wait_ge(self.sem, v)

    def close(self, rounds):
        self.base += rounds * self.per * self.by


def program(nc, x, src, dst, w0, b0, w_edge, w_node, b_node, w1, as1, ad1, b1, w2, as2, ad2, b2,
            wq, bq, wk, bk, wv, bv, wskip, bskip, out):
    N, D = x.shape
    E = src.shape[0]
    T = -(-E // P)
    NB = -(-N // P)
    NP = NB * P
    STEPS = T + NB - 1
    NG = -(-STEPS // G)
    SC = -(-(NG * G) // P)
    SP_ = SC * P
    QS = G // Q
    NGQ = -(-((STEPS + NB * (Q - 1)) // Q) // QS)
    SCQ = -(-(NGQ * G) // P)
    FULL, REST = N // P, N % P
    NBAT = NB // G
    HEADS1, HEADS3 = as1.shape[0], 2
    Q_SCALE = float(D // HEADS3) ** -0.5
    assert D == P and NB % G == 0 and REST and NG * G == STEPS and NG % RING == 0

    first_drams = {h: nc.dram_tensor(f"first_dram{h}", [SCQ * P * h, P], F32, kind="Internal").ap()
                   for h in (as1.shape[0], 2)}
    dst_pad = nc.dram_tensor("dst_pad", [(T + 1) * P], I32, kind="Internal").ap()
    src_pad = nc.dram_tensor("src_pad", [(T + 1) * P], I32, kind="Internal").ap()
    block_drams = [nc.dram_tensor(f"block_dram{k}", [c * P], I32, kind="Internal").ap() for k, c in enumerate((SC, SCQ))]
    tables = [nc.dram_tensor(f"table{i}", [NP, w], F32, kind="Internal").ap()
              for i, w in enumerate((D, D, D + HEADS1, D + HEADS1, 2 * D))]

    ctx = ExitStack()
    with ctx:
        def sb(name, shape, dt=F32):
            return ctx.enter_context(nc.sbuf_tensor(name, shape, dt))

        def sem(name):
            return ctx.enter_context(nc.semaphore(name))

        X = sb("X", [P, NB, D])
        acc = sb("acc", [P, NB + G, D + HEADS1])
        nodeQ = sb("nodeQ", [P, NB, 3, D], BF16)
        nodeD = sb("nodeD", [P, NB, 3, HEADS1], BF16)
        nodeM = sb("nodeM", [P, NB, HEADS1])
        deg = sb("deg", [P, NB, 1])
        srcT = [sb(f"srcT{k}", [P, c * P], I32) for k, c in enumerate((SC, SCQ))]
        slotT = [sb(f"slotT{k}", [P, c * P], BF16) for k, c in enumerate((SC, SCQ))]
        lastT = sb("lastT", [P, SCQ * P], BF16)
        blkq = sb("blkq", [1, SCQ * P // Q], I32)
        fresh = sb("fresh", [P, SCQ * P // Q])
        blk = sb("blk", [1, SP_], I32)
        blk_rel = sb("blk_rel", [1, SP_], I32)
        ident = sb("ident", [P, P])
        iota = sb("iota", [P, P])
        identb = sb("identb", [P, P], BF16)
        iotab = sb("iotab", [P, P], BF16)
        zerob = sb("zerob", [1, 512], BF16)
        GT = sb("GT", [P, RING, G, 2 * D])
        consts = sb("consts", [P, 3, 1])
        wbuf = sb("wbuf", [P, 3, 4 * D])
        bias = sb("bias", [P, 9, D])
        O = sb("O", [P, 2, G, P])
        Ob = sb("Ob", [P, RING, G, P], BF16)
        Ot = sb("Ot", [P, RING, G, P], BF16)
        V = sb("V", [P, 2, G, D + HEADS1])
        prod = sb("prod", [P, G, D])
        lg = sb("lg", [P, 2, G * HEADS1])
        lg2 = sb("lg2", [P, G * HEADS1])
        first = sb("first", [P, RING, P])
        seg = sb("seg", [P, 2, P])
        lastmax = sb("lastmax", [P, 2, G, HEADS1 + 1])
        lastmax1 = sb("lastmax1", [P, 2, G, HEADS1 + 1])
        lastmax2 = sb("lastmax2", [P, 2, G, HEADS1 + 1], BF16)
        tmax = sb("tmax", [P, 2, G, HEADS1])
        pen = sb("pen", [P, 2, G])
        qmax = sb("qmax", [P, 2, QS, HEADS1])
        oldM = sb("oldM", [P, 2, QS, HEADS1])
        newM = sb("newM", [P, 2, QS, HEADS1])
        newM1 = sb("newM1", [P, 2, QS, HEADS1])
        newM2 = sb("newM2", [P, 2, QS, HEADS1], BF16)
        diff = sb("diff", [P, 2, QS, HEADS1])
        resc = sb("resc", [P, 2, QS, HEADS1])
        below = sb("below", [P, 2, G * HEADS1])
        Y, Y2, YT = O[:, 0], O[:, 1], prod
        R = GT[:, 0, :, :]
        st = sb("st", [P, 4, G * HEADS1])

        psT = ctx.enter_context(nc.psum_tensor("psT", [P, G, P], BF16))
        psD = ctx.enter_context(nc.psum_tensor("psD", [P, G, P], F32))
        psS = ctx.enter_context(nc.psum_tensor("psS", [P, 512], F32))
        psA = ctx.enter_context(nc.psum_tensor("psA", [P, G, 256], F32))
        psN = psA[:, 0:G // 2, :].rearrange("p a (b e) -> p (a b) e", e=P)

        def top(ap):
            return ap.bitcast(BF16)[..., 1::2]

        apart_sem = sem("apart")

        def apart(eng):
            eng.sem_inc(apart_sem, 1)

        def thread_sems(name):
            return {kind: Signal(sem(f"{name}_{kind}"), 0, 16 if kind.endswith("dma") else 1)
                    for kind in ("compute", "sync_dma", "pool_dma")}

        THREADS = 4
        SPREAD = 6
        H = G // THREADS
        chain_sems = [thread_sems(f"chain{n}") for n in range(THREADS)]

        def chain(stages, rounds=1, threads=1, refill=None):
            stages = [stage if len(stage) == 3 else (*stage, 1) for stage in stages]
            kinds = [who if who.endswith("dma") else "compute" for who, _, _ in stages]
            places, count = [], dict.fromkeys(chain_sems[0], 0)
            for kind, (_, _, n) in zip(kinds, stages):
                count[kind] += n
                places.append(count[kind] - 1)
            for sems in chain_sems[:threads]:
                for kind, sg in sems.items():
                    sg.per = count[kind]
            with nc.Block() as block:
                def stage(eng, n, i, thread):
                    sems = chain_sems[thread]
                    who, fn, parts = stages[n]
                    if n:
                        sems[kinds[n - 1]].wait(eng, i, places[n - 1])
                    elif rounds > 1:
                        n_ = -1 if refill is None else -2
                        sems[kinds[n_]].wait(eng, i - 1, places[n_])
                    if n == refill:
                        sems[kinds[-1]].wait(eng, i - 1)
                    if rounds > 1 and kinds[n] == "compute":
                        apart(eng)
                    made = fn(eng, Part(i, thread) if threads > 1 else i)
                    made = made if isinstance(made, list) else [made]
                    assert len(made) == parts
                    for ins in made:
                        sems[kinds[n]].done(ins)

                def body(eng, key, i):
                    for n in range(len(stages)):
                        for thread in reversed(range(threads)):
                            m, j = n - thread * len(stages) // SPREAD, i
                            if m < 0:
                                m, j = m + len(stages), i - 1
                            if stages[m][0].split("_")[0] == key and not (isinstance(j, int) and j in (-1, rounds)):
                                stage(eng, m, j, thread)

                def run(key):
                    def _(eng):
                        if not any(who.split("_")[0] == key for who, _, _ in stages):
                            return
                        body(eng, key, 0)
                        if rounds > 1:
                            with eng.Fori(1, rounds) as i:
                                body(eng, key, i)
                            body(eng, key, rounds)
                    return _

                block.sync(run("sync"))
                block.gpsimd(run("pool"))
                block.scalar(run("scalar"))
                block.vector(run("vector"))
                block.tensor(run("tensor"))
            for sems in chain_sems[:threads]:
                for sg in sems.values():
                    sg.close(rounds)

        load_sem = sem("load")
        c_sem = sem("const")
        zrow, padrow = (acc[0:1, 2 * k:2 * k + 2, 0:P].bitcast(I32) for k in range(2))
        rowi = [t[0:1, :, :].rearrange("p g e -> p (g e)").bitcast(I32) for t in (O[:, 0], O[:, 1], prod)]
        work = nodeQ[:, :, :, :].rearrange("p b k f -> p (b k f)").bitcast(F32)
        vsb = [work[:, k * 1024:(k + 1) * 1024] for k in range(2)]
        row = [work[0:1, k * 1024:(k + 1) * 1024] for k in range(2, 5)]
        vall = psD[:, :, :].rearrange("p a b -> p (a b)")
        sidx_i = sb("sidx_i", [P, SCQ], I32)
        sidx = sb("sidx", [P, 6, SCQ])
        tb_i = sb("tb_i", [P, 2, SCQ], I32)
        bcol = sb("bcol", [P, 6])
        bcol_i = sb("bcol_i", [P, 1], I32)
        tri = sb("tri", [P, NB])
        brow = sb("brow", [P, 2, NB])
        bwork = work[:, 5 * 1024:5 * 1024 + 2 * SCQ * NB].rearrange("p (k c b) -> p k c b", k=2, c=SCQ)
        iota_i = sb("iota_i", [P, P], I32)
        hmask = sb("hmask", [P, HEADS1])
        acol = sb("acol", [P, 4])
        adiag = sb("adiag", [P, 4, HEADS1])
        wraw = V[:, :, :, :].rearrange("p a g e -> p (a g e)")[:, 0:10 * D].rearrange("p (k f) -> p k f", f=D)
        flat = GT[:, :, :, :].rearrange("p r g w -> p (r g w)")
        rows = [flat[:, i * SCQ * P:(i + 1) * SCQ * P].rearrange("p (c e) -> p c e", c=SCQ) for i in range(6)]
        assert 6 * SCQ * P + 2 * 1024 <= RING * G * 2 * D and T <= 1024
        edges_all = [flat[:, 6 * SCQ * P + k * 1024:6 * SCQ * P + k * 1024 + T] for k in range(2)]

        W0, WEA, WEB, WN, W1R, W2R, WQR, WKR, WVR, WSR = range(10)
        n_loads = 0
        with nc.Block() as block:
            @block.sync
            def _(eng):
                n = 0

                def load(to, of):
                    nonlocal n
                    eng.dma_start(to, of).then_inc(load_sem, 16)
                    n += 1

                load(X[:, 0:FULL, :], x[0:FULL * P, :].rearrange("(b p) f -> p b f", p=P))
                for slot, w in ((W0, w0), (WEA, w_edge[:, 0:D]), (WEB, w_edge[:, D:2 * D]),
                                (WN, w_node), (W1R, w1), (W2R, w2), (WQR, wq), (WKR, wk),
                                (WVR, wv), (WSR, wskip)):
                    load(wraw[:, slot, :], w)
                for k, b in enumerate((b0, b_node, b1, b2, bk, bv, bq, bskip)):
                    load(bias[:, k, :], b.rearrange("(a f) -> a f", a=1).to_broadcast([P, D]))
                for k, a in enumerate((as1, ad1, as2, ad2)):
                    load(acol[:, k:k + 1], a.rearrange("h (c o) -> (h c) o", o=1))
                load(dst_pad[0:E].rearrange("(a n) -> a n", a=8), dst.rearrange("(a n) -> a n", a=8))
                load(src_pad[0:E].rearrange("(a n) -> a n", a=8), src.rearrange("(a n) -> a n", a=8))
                eng.wait_ge(c_sem, 3)
                load(X[0:REST, FULL, :], x[FULL * P:N, :])
                load(dst_pad[E:(T + 1) * P].rearrange("(a k n) -> a k n", a=1, k=2), padrow[:, :, 0:((T + 1) * P - E) // 2])
                load(src_pad[E:(T + 1) * P].rearrange("(a k n) -> a k n", a=1, k=2), zrow[:, :, 0:((T + 1) * P - E) // 2])
                eng.wait_ge(load_sem, 16 * n)
                nonlocal n_loads
                n_loads = n

            @block.gpsimd
            def _(eng):
                eng.memset(zrow, 0).then_inc(c_sem, 1)
                eng.memset(padrow, 2 * NP).then_inc(c_sem, 1)
                eng.memset(X[:, FULL, :], 0.0).then_inc(c_sem, 1)
                eng.memset(ident[:, :], 0.0).then_inc(c_sem, 1)
                eng.memset(hmask[:, :], 1.0).then_inc(c_sem, 1)
                eng.memset(tri[:, :], 1.0).then_inc(c_sem, 1)
                for k, value in enumerate((0.0, 1.0, -BIG)):
                    eng.memset(consts[:, k, :], value).then_inc(c_sem, 1)
                eng.wait_ge(c_sem, 9)
                eng.affine_select(out=ident[:, :], in_=ident[:, :], compare_op=ALU.not_equal, fill=1.0,
                                  base=0, pattern=[[-1, P]], channel_multiplier=1).then_inc(c_sem, 1)
                eng.affine_select(out=tri[:, :], in_=tri[:, :], compare_op=ALU.is_ge, fill=0.0,
                                  base=-1, pattern=[[1, NB]], channel_multiplier=-1).then_inc(c_sem, 1)
                eng.affine_select(out=hmask[:, :], in_=hmask[:, :], compare_op=ALU.is_ge, fill=0.0,
                                  base=0, pattern=[[-(D // HEADS1), HEADS1]],
                                  channel_multiplier=1).then_inc(c_sem, 1)
                eng.wait_ge(c_sem, 12)
                eng.affine_select(out=hmask[:, :], in_=hmask[:, :], compare_op=ALU.is_ge, fill=0.0,
                                  base=D // HEADS1 - 1, pattern=[[D // HEADS1, HEADS1]],
                                  channel_multiplier=-1).then_inc(c_sem, 1)
                eng.iota(iota_i[:, :], pattern=[[1, P]], base=0, channel_multiplier=0).then_inc(c_sem, 1)
                eng.iota(sidx_i[:, :], pattern=[[P, SCQ]], base=0, channel_multiplier=1).then_inc(c_sem, 1)
                eng.iota(rowi[2][:, 0:T], pattern=[[1, T]], base=0, channel_multiplier=0).then_inc(c_sem, 1)

            @block.vector
            def _(eng):
                eng.wait_ge(c_sem, 16)
                eng.tensor_copy(iota[:, :], iota_i[:, :]).then_inc(c_sem, 1)
                eng.tensor_copy(iotab[:, :], iota_i[:, :]).then_inc(c_sem, 1)
                eng.tensor_copy(identb[:, :], ident[:, :]).then_inc(c_sem, 1)
                eng.memset(zerob[:, :], 0.0).then_inc(c_sem, 1)
                eng.memset(newM[:, :, :, :], -BIG).then_inc(c_sem, 1)
                eng.tensor_copy(sidx[:, 0, :], sidx_i[:, :]).then_inc(c_sem, 1)
                eng.tensor_copy(row[2][:, 0:T], rowi[2][:, 0:T]).then_inc(c_sem, 1)
                eng.wait_ge(load_sem, 16 * n_loads)
                for k in range(4):
                    eng.tensor_scalar(adiag[:, k, :], hmask[:, :], acol[:, k:k + 1], None, ALU.mult)\
                       .then_inc(c_sem, 1)

        shift, qshift = P.bit_length() - 1, Q.bit_length() - 1
        assert P == 1 << shift and Q == 1 << qshift
        e_rows = dst_pad.rearrange("(t e) -> t e", e=P)
        s_rows = src_pad.rearrange("(t e) -> t e", e=P)
        first_stored = sem("first_stored")
        st_ = []
        ones_row = sb("ones_row", [1, P])

        def add(who, fn, n=1):
            st_.append((who, fn, n))

        def vec(fn, n=1):
            add("vector", lambda e, i: fn(e), n)

        def edge_column(e, k):
            of = e_rows[0:T, 0:1] if k == 0 else e_rows[0:T, P - 1:P]
            return e.dma_start(rowi[k][:, 0:T], of.rearrange("t o -> o t"), allow_slow_non_contiguous=True)

        def spread(of, n):
            def _(e, i):
                for a in range(0, n, 512):
                    z = min(n, a + 512)
                    ins = e.matmul(vall[:, a:z], ones_row[0:1, :], of[:, a:z], start=True, stop=True)
                return ins
            add("tensor", _)

        add("sync_dma", lambda e, i: [edge_column(e, 0), edge_column(e, 1)], 2)
        vec(lambda e: e.memset(ones_row[:, :], 1.0))
        vec(lambda e: [e.tensor_copy(row[0][:, 0:T], rowi[0][:, 0:T]), e.tensor_copy(row[1][:, 0:T], rowi[1][:, 0:T])], 2)
        for k in range(2):
            spread(row[k], T)
            vec(lambda e, k=k: e.tensor_copy(edges_all[k], vall[:, 0:T]))

        def fetch(k, c_):
            def _(e, i):
                return [e.indirect_dma_start(out=rows[n][:, c, :].bitcast(I32), out_offset=None, in_=of,
                                             in_offset=bass.IndirectOffsetOnAxis(ap=tb_i[:, 0, c:c + 1], axis=0))
                        for c in range(c_) for n, of in enumerate((e_rows, s_rows))]
            add("pool_dma", _, 2 * c_)

        def turn(of, c_, to):
            def _(e, i):
                for c in range(c_):
                    ins = e.transpose(psN[:, c, :], of[:, c, :], ident[:, :])
                return ins
            add("tensor", _)
            vec(lambda e: e.tensor_copy(to[:, :], psN[:, 0:c_, :].rearrange("p c s -> p (c s)")))

        def tables_of_steps(k, c_):
            dst_f, src_f = rows[2][:, 0:c_, :], rows[3][:, 0:c_, :]
            vec(lambda e: e.tensor_scalar(sidx[:, 3, :], sidx[:, 2, :], float(P), None, ALU.mult))
            vec(lambda e: e.tensor_copy(tb_i[:, :, :], sidx[:, 1:3, :]))
            add("sync_dma", lambda e, i: e.dma_start(block_drams[k].rearrange("(c p) -> p c", p=P), tb_i[:, 1, 0:c_],
                                                     allow_slow_non_contiguous=True))
            fetch(k, c_)
            vec(lambda e: [e.tensor_copy(dst_f, rows[0][:, 0:c_, :].bitcast(I32)),
                           e.tensor_copy(src_f, rows[1][:, 0:c_, :].bitcast(I32))], 2)
            if k:
                last_r, first_r = rows[4][:, 0:c_, :], rows[5][:, 0:c_, :]
                vec(lambda e: [e.memset(last_r[:, :, P - 1:P], 1.0), e.memset(first_r[:, :, 0:1], -BIG),
                               e.tensor_tensor(last_r[:, :, 0:P - 1], dst_f[:, :, 0:P - 1], dst_f[:, :, 1:P],
                                               ALU.not_equal)], 3)
                vec(lambda e: e.tensor_scalar(first_r[:, :, 1:P], last_r[:, :, 0:P - 1], -BIG, None, ALU.mult))
                turn(last_r, c_, lastT)
            vec(lambda e: e.tensor_tensor(dst_f, dst_f, sidx[:, 3, 0:c_].unsqueeze(2).to_broadcast([P, c_, P]),
                                          ALU.subtract))
            turn(src_f, c_, srcT[k])
            turn(dst_f, c_, slotT[k])

        vec(lambda e: e.tensor_scalar(rowi[2][:, 0:T], rowi[0][:, 0:T], shift, None, ALU.logical_shift_right))
        vec(lambda e: e.tensor_copy(row[0][:, 0:T], rowi[2][:, 0:T]))
        vec(lambda e: e.tensor_tensor(row[0][:, 0:T], row[0][:, 0:T], row[2][:, 0:T], ALU.add))
        spread(row[0], T)
        vec(lambda e: e.tensor_copy(vsb[0][:, 0:T], vall[:, 0:T]))
        for c in range(SC):
            vec(lambda e, c=c: e.tensor_scalar(vsb[1][:, 0:T], vsb[0][:, 0:T], sidx[:, 0, c:c + 1], None,
                                               ALU.is_le, ALU.add, accum_out=sidx[:, 4, c:c + 1]))
        vec(lambda e: e.memset(sidx[:, 1, :], 0.0))
        vec(lambda e: e.tensor_scalar(sidx[:, 1, 0:SC], sidx[:, 4, 0:SC], -1.0, None, ALU.add))
        vec(lambda e: e.tensor_tensor(sidx[:, 2, :], sidx[:, 0, :], sidx[:, 1, :], ALU.subtract))
        tables_of_steps(0, SC)
        add("sync_dma", lambda e, i: e.dma_start(blk[:, :], block_drams[0].rearrange("(a s) -> a s", a=1)))
        blk_g, rel_g = (t[:, :].rearrange("p (g j) -> p g j", j=G) for t in (blk, blk_rel))
        vec(lambda e: e.tensor_tensor(rel_g, blk_g, blk_g[:, :, 0:1].to_broadcast([1, SP_ // G, G]), ALU.subtract))

        vec(lambda e: e.tensor_scalar(bcol[:, 0:1], sidx[:, 0, 0:1], float(P), None, ALU.mult))
        vec(lambda e: e.tensor_scalar(bcol[:, 1:2], bcol[:, 0:1], float(P), None, ALU.add))
        vec(lambda e: e.tensor_scalar(vsb[1][:, 0:T], edges_all[1], bcol[:, 0:1], None, ALU.is_lt, ALU.add,
                                      accum_out=bcol[:, 2:3]))
        vec(lambda e: e.tensor_scalar(vsb[1][:, 0:T], edges_all[0], bcol[:, 1:2], None, ALU.is_lt, ALU.add,
                                      accum_out=bcol[:, 3:4]))
        vec(lambda e: e.tensor_tensor(bcol[:, 4:5], bcol[:, 3:4], bcol[:, 2:3], ALU.subtract))
        vec(lambda e: e.tensor_scalar(bcol[:, 4:5], bcol[:, 4:5], 0.0, float(Q - 1), ALU.max, ALU.add))
        vec(lambda e: e.tensor_copy(bcol_i[:, :], bcol[:, 4:5]))
        vec(lambda e: e.tensor_scalar(bcol_i[:, :], bcol_i[:, :], qshift, None, ALU.logical_shift_right))
        vec(lambda e: e.tensor_copy(bcol[:, 5:6], bcol_i[:, :]))

        def block_rows(e, i):
            e.matmul(vall[:, 0:NB], bcol[:, 5:6].to_broadcast([P, P]), tri[:, :], start=True, stop=True)
            return e.matmul(vall[:, NB:2 * NB], bcol[:, 2:3].to_broadcast([P, P]), ident[:, 0:NB], start=True, stop=True)
        add("tensor", block_rows)
        vec(lambda e: e.tensor_scalar(brow[:, 0, :], vall[:, 0:NB], float(Q), None, ALU.mult))
        vec(lambda e: e.tensor_copy(brow[:, 1, :], vall[:, NB:2 * NB]))

        def by_step(ap):
            return ap.unsqueeze(2).to_broadcast([P, SCQ, NB])

        def by_block(ap):
            return ap.unsqueeze(1).to_broadcast([P, SCQ, NB])
        vec(lambda e: e.tensor_tensor(bwork[:, 0], by_block(brow[:, 0, :]), by_step(sidx[:, 0, :]), ALU.is_le))
        vec(lambda e: e.tensor_reduce(sidx[:, 2, :], bwork[:, 0], AX.X, ALU.add))
        vec(lambda e: e.tensor_scalar(sidx[:, 2, :], sidx[:, 2, :], -1.0, None, ALU.add))
        vec(lambda e: e.tensor_tensor(bwork[:, 0], by_block(iota[:, 0:NB]), by_step(sidx[:, 2, :]), ALU.is_equal))
        for k in range(2):
            vec(lambda e, k=k: e.tensor_tensor(bwork[:, 1], bwork[:, 0], by_block(brow[:, k, :]), ALU.mult))
            vec(lambda e, k=k: e.tensor_reduce(sidx[:, 4 + k, :], bwork[:, 1], AX.X, ALU.add))
        vec(lambda e: e.tensor_tensor(sidx[:, 1, :], sidx[:, 0, :], sidx[:, 4, :], ALU.subtract))
        vec(lambda e: e.tensor_tensor(sidx[:, 1, :], sidx[:, 1, :], sidx[:, 5, :], ALU.add))
        vec(lambda e: e.tensor_scalar(sidx[:, 1, :], sidx[:, 1, :], float(T), None, ALU.min))
        tables_of_steps(1, SCQ)
        NQ = SCQ * P // Q

        def load_blkq(e, i):
            ins = e.dma_start(
                blkq[:, :], block_drams[1].rearrange("(q j) -> q j", j=Q)[:, 0:1].rearrange("q o -> o q"),
                allow_slow_non_contiguous=True)
            for h, fd in first_drams.items():
                for k in range(h):
                    e.dma_start(fd.rearrange("(c s h) e -> s h c e", s=P, h=h)[:, k], rows[5][:, 0:SCQ, :])\
                     .then_inc(first_stored, 16)
            return ins
        add("sync_dma", load_blkq)
        vec(lambda e: e.tensor_copy(row[0][:, 0:NQ], blkq[:, :]))
        vec(lambda e: [e.memset(row[1][:, 0:1], 1.0),
                       e.tensor_tensor(row[1][:, 1:NQ], row[0][:, 1:NQ], row[0][:, 0:NQ - 1], ALU.not_equal)], 2)
        spread(row[1], NQ)
        vec(lambda e: e.tensor_scalar(fresh[:, :], vall[:, 0:NQ], -BIG, None, ALU.mult))

        WT0, WTE, WTN = wbuf[:, 0, 0:D], wbuf[:, 0, D:3 * D], wbuf[:, 0, 3 * D:4 * D]
        WG = [wbuf[:, 1, 0:D + 2 * HEADS1], wbuf[:, 1, 2 * D:3 * D + 2 * HEADS1]]
        WX = wbuf[:, 2, :]
        w1t, w2t = acc[:, 0, 0:D], acc[:, 1, 0:D]

        def turn_w(e, i):
            for k, slot in enumerate((W0, WEA, WEB, WN, W1R, W2R)):
                ins = e.transpose(psN[:, k, :], wraw[:, slot, :], ident[:, :])
            return ins
        add("tensor", turn_w)
        add("vector", lambda e, i: e.tensor_copy(wbuf[:, 0, :].rearrange("p (k f) -> p k f", f=D), psN[:, 0:4, :]))
        add("vector", lambda e, i: e.tensor_copy(acc[:, 0:2, 0:D], psN[:, 4:6, :]))

        def w_by_a(e, i):
            for k, wt in enumerate((w1t, w2t)):
                ins = e.matmul(psS[:, 64 * k:64 * k + 2 * HEADS1], wt,
                               adiag[:, 2 * k:2 * k + 2, :].rearrange("p a h -> p (a h)"), start=True, stop=True)
            return ins
        add("tensor", w_by_a)
        for k, slot in enumerate((W1R, W2R)):
            add("vector", lambda e, i, k=k: e.tensor_copy(WG[k][:, D:D + 2 * HEADS1], psS[:, 64 * k:64 * k + 2 * HEADS1]))
            add("vector", lambda e, i, k=k, slot=slot: e.tensor_copy(WG[k][:, 0:D], wraw[:, slot, :]))
        for k, slot in enumerate((WKR, WVR, WQR, WSR)):
            add("vector", lambda e, i, k=k, slot=slot: e.tensor_copy(WX[:, k * D:(k + 1) * D], wraw[:, slot, :]))
        vec(lambda e: e.tensor_scalar(bias[:, 6, :], bias[:, 6, :], Q_SCALE, None, ALU.mult))
        add("vector", lambda e, i: e.memset(acc[:, NB:NB + G, :], 0.0))
        chain(st_)

        DH = D + HEADS1

        class Part:

            def __init__(self, i, thread):
                self.first = i * G + thread * H
                mine = slice(thread * H, (thread + 1) * H)
                self.Y, self.Y2, self.YT, self.R = (t[:, mine, :] for t in (Y, Y2, YT, R))
                self.rest = V[:, 0, mine, 0:D]
                self.ps = psA[:, mine, :]
                self.turned = self.ps[:, :, 0:P]
                self.st = [st[:, k, thread * H * HEADS1:(thread + 1) * H * HEADS1] for k in range(3)]

            def at(self, t):
                return t[:, bass.ds(self.first, H), :]

        def const(k, n):
            return consts[:, k:k + 1, :].to_broadcast([P, H, n])

        def wide(ap, n):
            return ap.unsqueeze(len(ap.shape)).to_broadcast([*ap.shape, n])

        def heads(ap, h):
            return ap.rearrange("p g (h c) -> p g h c", h=h)

        def refills(stage):
            return (*stage, 1, "refill")

        def node_phase(stages, table=None, rows_of=None):
            refill = [n for n, stage in enumerate(stages) if len(stage) > 3]
            stages = [stage[:3] for stage in stages]
            if table is not None:
                stages = stages + [("sync_dma", lambda e, n: e.dma_start(
                    n.at(table.rearrange("(b p) f -> p b f", p=P)), rows_of(n)[:, :, 0:table.shape[1]]))]
            chain(stages, NBAT, THREADS, *refill)

        def norm_stages(mark=lambda stage: stage):
            return [
                ("vector", lambda e, n: e.tensor_reduce(n.st[0][:, 0:H], n.at(X), AX.X, ALU.add)),
                mark(("vector", lambda e, n: e.scalar_tensor_tensor(
                    out=n.Y, in0=wide(n.st[0][:, 0:H], D), scalar=-1.0 / D, in1=n.at(X), op0=ALU.mult, op1=ALU.add))),
                ("scalar", lambda e, n: e.activation(n.Y2, n.Y, ACT.Square)),
                ("vector", lambda e, n: e.tensor_reduce(n.st[1][:, 0:H], n.Y2, AX.X, ALU.add)),
                ("vector", lambda e, n: e.tensor_scalar(n.st[1][:, 0:H], n.st[1][:, 0:H], 1.0 / D, LN_EPS,
                                                        ALU.mult, ALU.add)),
                ("scalar", lambda e, n: e.activation(n.st[2][:, 0:H], n.st[1][:, 0:H], ACT.Sqrt)),
                ("vector", lambda e, n: e.reciprocal(n.st[1][:, 0:H], n.st[2][:, 0:H])),
                ("vector", lambda e, n: e.scalar_tensor_tensor(
                    out=n.Y, in0=n.Y, scalar=0.0, in1=wide(n.st[1][:, 0:H], D), op0=ALU.max, op1=ALU.mult)),
            ]

        def turn_stages():
            def turn_y(e, n):
                for g in range(H):
                    ins = e.transpose(n.turned[:, g, :], n.Y[:, g, :], ident[:, :])
                return ins
            return [("tensor", turn_y), ("scalar", lambda e, n: e.copy(n.YT, n.turned))]

        def product(w):
            def mm(e, n):
                for g in range(H):
                    ins = e.matmul(n.ps[:, g, 0:w.shape[1]], n.YT[:, g, :], w, start=True, stop=True)
                return ins
            return ("tensor", mm)

        def bias_row(k, width=1):
            return bias[:, k:k + width, :].rearrange("p k f -> p (k f)").unsqueeze(1).to_broadcast([P, H, width * D])

        def plus_bias(to, k, width=1, c=0):
            return ("vector", lambda e, n: e.tensor_tensor(to(n), n.ps[:, :, c:c + width * D], bias_row(k, width),
                                                           ALU.add))

        def split_stages(of, to):
            def rest(n):
                return n.rest[:, :, 0:of(n).shape[-1]]
            return [
                ("scalar", lambda e, n: e.copy(n.at(to)[:, :, 0, :], top(of(n)))),
                ("vector", lambda e, n: e.tensor_tensor(rest(n), of(n), top(of(n)), ALU.subtract)),
                ("scalar", lambda e, n: e.copy(n.at(to)[:, :, 1, :], top(rest(n)))),
                ("vector", lambda e, n: e.tensor_tensor(n.at(to)[:, :, 2, :], rest(n), top(rest(n)), ALU.subtract)),
            ]

        x_plus_y = ("vector", lambda e, n: e.tensor_tensor(n.at(X), n.at(X), n.Y, ALU.add))
        clear_acc = ("scalar", lambda e, n: e.copy(n.at(acc), const(0, DH)))

        def mean_stages(w, k, relu):
            return [
                ("vector", lambda e, n: e.reciprocal(n.st[0][:, 0:H], n.st[1][:, 0:H])),
                ("vector", lambda e, n: e.tensor_tensor(n.Y, n.at(acc)[:, :, 0:D], wide(n.st[0][:, 0:H], D), ALU.mult)),
                clear_acc, *turn_stages(), product(w), plus_bias(lambda n: n.Y, k),
                ("vector", lambda e, n: e.scalar_tensor_tensor(
                    out=n.at(X), in0=n.Y, scalar=0.0, in1=n.at(X), op0=ALU.max, op1=ALU.add)) if relu else x_plus_y,
            ]

        def softmax_stages(h, op, eps):
            c = D // h

            def sums(n):
                return n.at(acc)[:, :, 0:D + h].rearrange("p g (h c) -> p g h c", h=h)

            def den(n):
                return n.st[0][:, 0:H * h].rearrange("p (g h) -> p g h", h=h)
            return [
                ("vector", lambda e, n: e.tensor_scalar(den(n).unsqueeze(3), sums(n)[:, :, :, c:c + 1], eps, None, op)),
                ("vector", lambda e, n: e.reciprocal(den(n), den(n))),
                ("vector", lambda e, n: e.tensor_tensor(heads(n.Y, h), sums(n)[:, :, :, 0:c], wide(den(n), c), ALU.mult)),
            ]

        def gat_stages(wg):
            d0 = D + HEADS1
            c = D // HEADS1
            return [
                product(wg),
                refills(("scalar", lambda e, n: e.copy(n.R[:, :, 0:d0 + HEADS1], n.ps[:, :, 0:d0 + HEADS1]))),
                ("vector", lambda e, n: e.tensor_tensor(n.Y2[:, :, 0:HEADS1], n.R[:, :, D:d0], n.R[:, :, d0:d0 + HEADS1],
                                                        ALU.add)),
                ("vector", lambda e, n: e.scalar_tensor_tensor(
                    out=n.at(nodeM), in0=n.Y2[:, :, 0:HEADS1], scalar=0.2, in1=n.Y2[:, :, 0:HEADS1],
                    op0=ALU.mult, op1=ALU.max)),
                *split_stages(lambda n: n.R[:, :, d0:d0 + HEADS1], nodeD),
                ("scalar", lambda e, n: e.copy(n.at(acc), const(1, DH))),
                ("vector", lambda e, n: e.tensor_copy(heads(n.at(acc), HEADS1)[:, :, :, 0:c],
                                                      heads(n.R[:, :, 0:D], HEADS1))),
            ]

        signals = {}
        names = ("index", "staged", "onehot", "onehot32", "turned", "onehotT", "toedge", "prod", "head", "logit",
                 "logitT", "seg", "segT", "nmax", "pen", "tmax", "qmax", "drop", "resc", "lastmax1", "lastmax2", "newM1", "newM2", "maxedge", "below", "bound",
                 "weight", "values", "sums", "added")
        for n in names:
            signals[n] = Signal(sem(n))
        for n, per in (("lastmax", 2), ("mmax", 2 * QS), ("qscaled", QS), ("qadded", QS)):
            signals[n] = Signal(sem(n), per)
        ring_rows = [Signal(sem(f"rows{r}"), 1, 16 * G) for r in range(RING)]
        ring_first = [Signal(sem(f"first{r}"), 1, 16) for r in range(RING)]
        with nc.Block() as block:
            @block.gpsimd
            def _(eng):
                for sg in signals.values():
                    sg.base = RING * sg.per
                    eng.sem_inc(sg.sem, sg.base)

        def wait(name, eng, g, k=None):
            signals[name].wait(eng, g, k)

        used = set()

        def done(name, ins):
            used.add(name)
            signals[name].done(ins)

        def at_block(t, b, w):
            return t[:, bass.ds(b, 1), 0:w].rearrange("p o w -> p (o w)")

        def at_part(t, b, part):
            return t[:, bass.ds(b, 1), part, :].rearrange("p o w -> p (o w)")

        def table_ready(eng):
            for sems in chain_sems:
                eng.wait_ge(sems["sync_dma"].sem, sems["sync_dma"].base)

        reg_sets = {}

        def loaded(eng, which, table, g, n, most):
            if (eng.engine, which) not in reg_sets:
                reg_sets[eng.engine, which] = [eng.alloc_register(f"{which}_{j}") for j in range(n)]
            regs = reg_sets[eng.engine, which]
            eng.load(regs, table[0:1, bass.ds(g * n, n)])
            return [eng.snap(r, min_val=0, max_val=most) for r in regs]

        def over_groups(eng, n, turn, ahead=0):
            last = (n - ahead) // RING
            for k in range(RING):
                turn(0, k, k)
            with eng.Fori(1, last) as i:
                for k in range(RING):
                    turn(i, k, i * RING + k)
            for g in range(last * RING, n):
                turn(g // RING, g % RING, g)

        def next_of(i, k, n=1):
            return (i, k + n) if k + n < RING else (i + 1, k + n - RING)

        def previous(i, k, n=1):
            return (i, k - n) if k >= n else (i - 1, k - n + RING)

        def there(g, n):
            return not isinstance(g, int) or g < n

        def fetch_rows(eng, table, k, g, release):
            wait(release, eng, g - RING)
            wait("index", eng, g)
            table_ready(eng)
            apart(eng)
            for j in range(G):
                eng.indirect_dma_start(
                    out=GT[:, k, j, 0:table.shape[1]], out_offset=None, in_=table,
                    in_offset=bass.IndirectOffsetOnAxis(ap=srcI[:, k, j:j + 1], axis=0),
                ).then_inc(ring_rows[k].sem, 16)

        def copy_index(eng, steps, i, k, g):
            if not (isinstance(i, int) and i == 0):
                ring_rows[k].wait(eng, i - 1)
            done("index", eng.copy(srcI[:, k, :], srcT[steps][:, bass.ds(g * G, G)]))

        def one_hot(eng, out_, steps, g):
            return eng.tensor_tensor(out_, iotab[:, :].unsqueeze(1).to_broadcast([P, G, P]),
                                     wide(slotT[steps][:, bass.ds(g * G, G)], P), ALU.is_equal)

        def run_pass(n, parts, pool_release, table, sync=None):
            ahead = {"AA": 2, "A": 1, "B": 0, "C": -1, "CC": -2, "I": RING}

            def run(eng, own):
                look = max(ahead[what] for what, _ in own)
                for what, fn in sorted(own, key=lambda part: -ahead[part[0]]):
                    for g in range(ahead[what]):
                        fn(eng, g // RING, g % RING, g)

                def turn(i, k, g):
                    for what, fn in own:
                        n_ = ahead[what]
                        if n_ < 0:
                            if isinstance(g, int) and g + n_ < 0:
                                continue
                            ii, kk = previous(i, k, -n_)
                        elif n_ == RING:
                            ii, kk = i + 1, k
                        else:
                            ii, kk = next_of(i, k, n_)
                        if there(g + n_, n):
                            fn(eng, ii, kk, g + n_)
                over_groups(eng, n, turn, look)
                for end in range(n, n + 2):
                    for what, fn in own:
                        g = end + ahead[what]
                        if g < n:
                            fn(eng, g // RING, g % RING, g)

            with nc.Block() as block:
                @block.gpsimd
                def _(eng):
                    over_groups(eng, n, lambda i, k, g: fetch_rows(eng, table, k, g, pool_release))

                @block.sync
                def _(eng):
                    if sync:
                        over_groups(eng, n, lambda i, k, g: sync(eng, i, k, g))

                @block.scalar
                def _(eng):
                    run(eng, parts["scalar"])

                @block.tensor
                def _(eng):
                    run(eng, parts["tensor"])

                @block.vector
                def _(eng):
                    table_ready(eng)
                    run(eng, parts["vector"])

            for name in used:
                signals[name].close(n)
            used.clear()
            for k in range(RING):
                for r in (ring_rows, ring_first) if sync else (ring_rows,):
                    r[k].close(-(-(n - k) // RING))

        def sum_pass(kind, table):
            mlp = kind == "mlp"
            VW = D if mlp else D + 1
            dve_b = {}

            def act_A(eng, i, k, g):
                q = k % 2
                wait("onehot", eng, g)
                wait("sums", eng, g - 2)
                done("onehot32", eng.copy(O[:, q, :, :], Ob[:, q, :, :]))
                wait("turned", eng, g)
                wait("toedge", eng, g - 2)
                done("onehotT", eng.copy(Ot[:, q, :, :], psT[:, :, :]))

            def act_relu(eng, i, k, g):
                wait("prod", eng, g)
                wait("sums", eng, g - 2)
                done("values", eng.activation(V[:, k % 2, :, 0:D], prod[:, :, :], ACT.Relu))

            def pe_A(eng, i, k, g):
                q = k % 2
                wait("onehot", eng, g)
                wait("onehotT", eng, g - 1)
                for j in range(G):
                    ins = eng.transpose(psT[:, j, :], Ob[:, q, j, :], identb[:, :])
                done("turned", ins)
                b = loaded(eng, "blocks", blk, g, G, NB - 1)
                wait("onehotT", eng, g)
                wait("prod", eng, g - 1)
                for j in range(G):
                    for part in range(3):
                        ins = eng.matmul(psD[:, j, :], Ot[:, q, j, :], at_part(nodeQ, b[j], part), start=part == 0,
                                         stop=part == 2)
                done("toedge", ins)

            def pe_B(eng, i, k, g):
                q = k % 2
                if mlp:
                    wait("values", eng, g)
                else:
                    ring_rows[k].wait(eng, i)
                wait("onehot32", eng, g)
                wait("added", eng, g - 1)
                place = loaded(eng, "places", blk_rel, g, G, G - 1)
                for n in range(0, G, 2):
                    eng.matmul(psA[:, n:n + 2, 0:VW], zerob[0:1, 0:P], zerob[0:1, 0:2 * VW], start=True, stop=False,
                               skip_group_check=True)
                for j in range(G):
                    val = V[:, q, j, 0:VW] if mlp else GT[:, k, j, 0:VW]
                    to = psA[:, bass.ds(place[j], 1), 0:VW].rearrange("p o w -> p (o w)")
                    ins = eng.matmul(to, O[:, q, j, :], val, start=False, stop=j == G - 1, skip_group_check=True)
                done("sums", ins)

            def dve_A(eng, i, k, g):
                if mlp:
                    wait("turned", eng, g - 2)
                    wait("onehot32", eng, g - 2)
                    done("onehot", one_hot(eng, Ob[:, k % 2, :, :], 0, g))
                else:
                    wait("sums", eng, g - 2)
                    done("onehot32", one_hot(eng, O[:, k % 2, :, :], 0, g))

            def dve_prod(eng, i, k, g):
                ring_rows[k].wait(eng, i)
                wait("toedge", eng, g)
                wait("values", eng, g - 1)
                done("prod", eng.tensor_tensor(prod[:, :, :], psD[:, :, :], GT[:, k, :, 0:D], ALU.add))

            def dve_C(eng, i, k, g):
                b = loaded(eng, "blocks", blk, g, G, NB - 1)
                a = acc[:, bass.ds(b[0], G), 0:VW]
                wait("sums", eng, g)
                wait("added", eng, g - 1)
                done("added", eng.tensor_tensor(a, a, psA[:, :, 0:VW], ALU.add))

            index = ("I", lambda eng, i, k, g: copy_index(eng, 0, i, k, g))
            run_pass(NG, {
                "scalar": (("A", act_A), index, ("A", act_relu)) if mlp else (index,),
                "tensor": (("A", pe_A), ("B", pe_B)) if mlp else (("B", pe_B),),
                "vector": (("A", dve_A), ("C", dve_C), ("A", dve_prod)) if mlp else (("A", dve_A), ("C", dve_C)),
            }, "prod" if mlp else "sums", table)

        srcI = sb("srcI", [P, RING, G], I32)
        quantD = sb("quantD", [P, 2, QS, 3, D], BF16)
        quantZ = sb("quantZ", [P, 2, QS, HEADS1])
        quantF = sb("quantF", [P, 2, QS])

        def softmax_pass(kind, table, h):
            gat = kind == "gat"
            HG, C = h * G, D // h
            VW = D + h
            f0 = 0 if gat else D
            dw = h if gat else D
            flatA = psA[:, :, :].rearrange("p g w -> p (g w)")
            assert 4 * QS * 256 <= 1024 * 2
            logT, segR = flatA[0:HG, 1024:1024 + P], flatA[:, 1024 + P:1024 + P + HG]
            maxima = psS[:, 0:G * (h + 1)].rearrange("p (g w) -> p g w", g=G)
            edge_max = psS[:, 256:256 + HG].rearrange("p (g h) -> p g h", g=G)

            def by_head(ap):
                return ap.rearrange("p (g h) -> p g h", g=G)

            def first_rows(eng, i, k, g):
                wait("seg", eng, g - RING)
                ring_first[k].done(eng.dma_start(first[0:HG, k, :], first_drams[h][bass.ds(g * HG, HG), :]))

            def stage(eng, i, k, g):
                q = k % 2
                b = loaded(eng, f"quanta{q}", blkq, g, QS, NB - 1)
                wait("toedge", eng, g - 2)
                wait("mmax", eng, g - 2)
                for u in range(QS):
                    eng.copy(quantD[:, q, u, :, 0:dw], (nodeD if gat else nodeQ)[:, bass.ds(b[u], 1), :, :]
                             .rearrange("p o k w -> p (o k) w"))
                    eng.copy(quantZ[:, q, u, 0:h], at_block(nodeM, b[u], h))
                done("staged", eng.copy(quantF[:, q, :], fresh[:, bass.ds(g * QS, QS)]))

            def act_turned(eng, i, k, g):
                wait("turned", eng, g)
                wait("maxedge", eng, g - RING)
                done("onehotT", eng.copy(Ot[:, k, :, :], psT[:, :, :]))

            def act_onehot32(eng, i, k, g):
                wait("onehot", eng, g)
                wait("sums", eng, g - 2)
                done("onehot32", eng.copy(O[:, k % 2, :, :], Ob[:, k, :, :]))

            def act_resc(eng, i, k, g):
                q = k % 2
                wait("drop", eng, g)
                wait("qadded", eng, g - 2)
                done("resc", eng.activation(resc[:, q, 0:QS, 0:h], diff[:, q, 0:QS, 0:h], ACT.Exp))

            def act_weight(eng, i, k, g):
                q = k % 2
                wait("bound", eng, g)
                wait("sums", eng, g - 2)
                v = V[:, q, :, 0:VW].rearrange("p g (h c) -> p g h c", h=h)
                done("weight", eng.activation(v[:, :, :, C:C + 1], by_head(below[:, q, 0:HG]).unsqueeze(3), ACT.Exp))

            def pe_turn(eng, i, k, g):
                wait("onehot", eng, g)
                wait("onehotT", eng, g - 1)
                for j in range(G):
                    ins = eng.transpose(psT[:, j, :], Ob[:, k, j, :], identb[:, :])
                done("turned", ins)

            def pe_toedge(eng, i, k, g):
                q = k % 2
                wait("staged", eng, g)
                wait("onehotT", eng, g)
                wait("prod", eng, g - 1)
                for j in range(G):
                    for part in range(3):
                        ins = eng.matmul(psD[:, j, 0:dw], Ot[:, k, j, :], quantD[:, q, j // Q, part, 0:dw],
                                         start=part == 0, stop=part == 2)
                done("toedge", ins)

            def pe_logitT(eng, i, k, g):
                wait("logit", eng, g)
                wait("lastmax", eng, g - 1)
                done("logitT", eng.transpose(logT, lg[:, k % 2, 0:HG], ident[:, :]))

            def pe_segT(eng, i, k, g):
                wait("seg", eng, g)
                if HG < P:
                    apart(eng)
                done("segT", eng.transpose(segR, seg[0:HG, k % 2, :], ident[0:HG, 0:HG]))

            def pe_maxima(eng, i, k, g):
                q = k % 2
                wait("onehot", eng, g)
                wait("lastmax2", eng, g)
                wait("below", eng, g - 1)
                for j in range(G):
                    for n, part in enumerate((top(lastmax[:, q, j, 0:h + 1]), top(lastmax1[:, q, j, 0:h + 1]),
                                              lastmax2[:, q, j, 0:h + 1])):
                        ins = eng.matmul(maxima[:, j, :], Ob[:, k, j, :], part, start=n == 0, stop=n == 2)
                done("nmax", ins)

            def pe_maxedge(eng, i, k, g):
                q = k % 2
                wait("newM2", eng, g)
                for j in range(G):
                    u = j // Q
                    for n, part in enumerate((top(newM[:, q, u, 0:h]), top(newM1[:, q, u, 0:h]), newM2[:, q, u, 0:h])):
                        ins = eng.matmul(edge_max[:, j, :], Ot[:, k, j, :], part, start=n == 0, stop=n == 2)
                done("maxedge", ins)

            def pe_sums(eng, i, k, g):
                q = k % 2
                wait("values", eng, g)
                wait("onehot32", eng, g)
                wait("qadded", eng, g - 2)
                for j in range(G):
                    ins = eng.matmul(psA[:, q * QS + j // Q, 0:VW], O[:, q, j, :], V[:, q, j, 0:VW],
                                     start=j % Q == 0, stop=j % Q == Q - 1)
                done("sums", ins)

            def dve_onehot(eng, i, k, g):
                wait("nmax", eng, g - RING)
                wait("turned", eng, g - RING)
                wait("onehot32", eng, g - RING)
                done("onehot", one_hot(eng, Ob[:, k, :, :], 1, g))

            def dve_prod(eng, i, k, g):
                ring_rows[k].wait(eng, i)
                wait("toedge", eng, g)
                if gat:
                    done("prod", eng.tensor_tensor(by_head(lg2[:, 0:HG]), psD[:, :, 0:h], GT[:, k, :, D:D + h], ALU.add))
                else:
                    done("prod", eng.tensor_tensor(prod[:, :, :], psD[:, :, :], GT[:, k, :, 0:D], ALU.mult))

            def dve_logit(eng, i, k, g):
                q = k % 2
                wait("prod", eng, g)
                wait("below", eng, g - 2)
                if gat:
                    done("logit", eng.scalar_tensor_tensor(
                        out=lg[:, q, 0:HG], in0=lg2[:, 0:HG], scalar=0.2, in1=lg2[:, 0:HG],
                        op0=ALU.mult, op1=ALU.max))
                else:
                    done("logit", eng.tensor_reduce(
                        lg[:, q, 0:HG], prod[:, :, :].rearrange("p g (h c) -> p (g h) c", h=h), AX.X, ALU.add))

            def dve_seg(eng, i, k, g):
                wait("logitT", eng, g)
                ring_first[k].wait(eng, i)
                wait("segT", eng, g - 2)
                done("seg", eng.tensor_tensor_scan(seg[0:HG, k % 2, :], first[0:HG, k, :], logT, -BIG, ALU.add, ALU.max))

            def dve_lastmax(eng, i, k, g):
                q = k % 2
                wait("segT", eng, g)
                wait("nmax", eng, g - 2)
                last = lastT[:, bass.ds(g * G, G)]
                done("lastmax", eng.tensor_tensor(lastmax[:, q, :, 0:h], by_head(segR), wide(last, h), ALU.mult))
                done("lastmax", eng.tensor_copy(lastmax[:, q, :, h:h + 1], last.unsqueeze(2)))
                of, rest = lastmax[:, q, :, 0:h + 1], lastmax1[:, q, :, 0:h + 1]
                wait("lastmax", eng, g)
                done("lastmax1", eng.tensor_tensor(rest, of, top(of), ALU.subtract))
                wait("lastmax1", eng, g)
                done("lastmax2", eng.tensor_tensor(lastmax2[:, q, :, 0:h + 1], rest, top(rest), ALU.subtract))

            def before(eng, i, k, g, u):
                q = k % 2
                if u:
                    wait("mmax", eng, g, 2 * u - 1)
                else:
                    wait("staged", eng, g)
                    wait("drop", eng, g - 2)
                    wait("mmax", eng, g - 1)
                last = newM[:, q, u - 1, 0:h] if u else newM[:, 1 - q, QS - 1, 0:h]
                done("mmax", eng.scalar_tensor_tensor(
                    out=oldM[:, q, u, 0:h], in0=last, scalar=quantF[:, q, u:u + 1], in1=quantZ[:, q, u, 0:h],
                    op0=ALU.add, op1=ALU.max))

            def after(eng, i, k, g, u):
                q = k % 2
                wait("mmax", eng, g, 2 * u)
                if not u:
                    wait("maxedge", eng, g - 2)
                    wait("qmax", eng, g)
                done("mmax", eng.tensor_tensor(newM[:, q, u, 0:h], oldM[:, q, u, 0:h], qmax[:, q, u, 0:h], ALU.max))

            def dve_before(eng, i, k, g):
                before(eng, i, k, g, 0)

            def dve_pen(eng, i, k, g):
                wait("nmax", eng, g)
                done("pen", eng.tensor_scalar(pen[:, k % 2, :].unsqueeze(2), maxima[:, :, h:h + 1], BIG, -BIG,
                                              ALU.mult, ALU.add))

            def dve_tmax(eng, i, k, g):
                q = k % 2
                wait("pen", eng, g)
                done("tmax", eng.tensor_tensor(tmax[:, q, :, 0:h], maxima[:, :, 0:h], wide(pen[:, q, :], h), ALU.add))

            def dve_qmax(eng, i, k, g):
                q = k % 2
                wait("tmax", eng, g)
                done("qmax", eng.tensor_reduce(qmax[:, q, :, 0:h], tmax[:, q, :, 0:h].rearrange("p (u j) h -> p u h j", j=Q),
                                               AX.X, ALU.max))

            def dve_max(eng, i, k, g):
                q = k % 2
                after(eng, i, k, g, 0)
                for u in range(1, QS):
                    before(eng, i, k, g, u)
                    after(eng, i, k, g, u)
                wait("mmax", eng, g)
                of, rest = newM[:, q, :, 0:h], newM1[:, q, :, 0:h]
                done("newM1", eng.tensor_tensor(rest, of, top(of), ALU.subtract))
                wait("resc", eng, g - 2)
                done("drop", eng.tensor_tensor(diff[:, q, 0:QS, 0:h], oldM[:, q, 0:QS, 0:h], newM[:, q, :, 0:h],
                                               ALU.subtract))
                wait("newM1", eng, g)
                done("newM2", eng.tensor_tensor(newM2[:, q, :, 0:h], rest, top(rest), ALU.subtract))

            def dve_below(eng, i, k, g):
                q = k % 2
                wait("maxedge", eng, g)
                wait("weight", eng, g - 2)
                done("below", eng.tensor_tensor(by_head(below[:, q, 0:HG]), by_head(lg[:, q, 0:HG]), edge_max,
                                                ALU.subtract))
                wait("below", eng, g)
                done("bound", eng.tensor_scalar(below[:, q, 0:HG], below[:, q, 0:HG], 0.0, None, ALU.min))

            def dve_values(eng, i, k, g):
                wait("weight", eng, g)
                v = V[:, k % 2, :, 0:VW].rearrange("p g (h c) -> p g h c", h=h)
                done("values", eng.tensor_tensor(
                    v[:, :, :, 0:C], heads(GT[:, k, :, f0:f0 + D], h),
                    v[:, :, :, C:C + 1].to_broadcast([P, G, h, C]), ALU.mult))

            def scale_sums(eng, i, k, g, u):
                a = at_block(acc, blocks[u], VW).rearrange("p (h c) -> p h c", h=h)
                wait("resc", eng, g)
                wait("qadded", eng, g if u else g - 1, u - 1 if u else None)
                done("qscaled", eng.tensor_tensor(a, a, wide(resc[:, k % 2, u, 0:h], C + 1), ALU.mult))

            def add_sums(eng, i, k, g, u):
                a = at_block(acc, blocks[u], VW)
                wait("sums", eng, g)
                wait("qscaled", eng, g, u)
                done("qadded", eng.tensor_tensor(a, a, psA[:, k % 2 * QS + u, 0:VW], ALU.add))

            def dve_scale(eng, i, k, g):
                blocks[:] = loaded(eng, "quanta", blkq, g, QS, NB - 1)
                scale_sums(eng, i, k, g, 0)

            def dve_add(eng, i, k, g):
                add_sums(eng, i, k, g, 0)
                for u in range(1, QS):
                    scale_sums(eng, i, k, g, u)
                    add_sums(eng, i, k, g, u)

            blocks = []
            index = ("I", lambda eng, i, k, g: copy_index(eng, 1, i, k, g))
            run_pass(NGQ, {
                "scalar": (index, ("B", act_resc), ("AA", act_turned), ("B", act_weight), ("AA", stage),
                           ("B", act_onehot32)),
                "tensor": (("B", pe_maxima), ("A", pe_toedge), ("AA", pe_turn), ("A", pe_logitT), ("B", pe_maxedge),
                           ("A", pe_segT), ("C", pe_sums)),
                "vector": (("AA", dve_onehot), ("B", dve_before), ("B", dve_pen), ("A", dve_prod), ("B", dve_tmax),
                           ("A", dve_logit), ("B", dve_qmax), ("B", dve_max), ("CC", dve_scale), ("A", dve_seg),
                           ("CC", dve_add), ("B", dve_below), ("A", dve_lastmax), ("B", dve_values)),
            } if gat else {
                "scalar": (index, ("AA", act_turned), ("AA", stage), ("B", act_weight), ("B", act_resc),
                           ("B", act_onehot32)),
                "tensor": (("B", pe_maxima), ("AA", pe_turn), ("A", pe_logitT), ("B", pe_maxedge),
                           ("A", pe_segT), ("AA", pe_toedge), ("C", pe_sums)),
                "vector": (("AA", dve_onehot), ("A", dve_prod), ("A", dve_logit), ("B", dve_before), ("B", dve_pen),
                           ("B", dve_tmax), ("B", dve_qmax), ("B", dve_max), ("CC", dve_scale), ("A", dve_seg),
                           ("CC", dve_add), ("B", dve_below), ("A", dve_lastmax), ("B", dve_values)),
            }, "values", table, first_rows)

        T0, T1, T2, T3, T4 = tables
        node_phase([clear_acc, *norm_stages(refills)], T0, lambda n: n.Y)
        with nc.Block() as block:
            @block.vector
            def _(eng):
                eng.wait_ge(first_stored, 16 * sum(first_drams))
                eng.memset(GT[:, :, :, D:D + 1], 1.0)
        sum_pass("sum", T0)

        node_phase([
            ("vector", lambda e, n: e.tensor_copy(n.at(deg), n.at(acc)[:, :, D:D + 1])),
            ("vector", lambda e, n: e.tensor_scalar(n.st[1][:, 0:H].unsqueeze(2), n.at(deg), MEAN_EPS, None, ALU.add)),
            *mean_stages(WT0, 0, False), *norm_stages(), *turn_stages(),
            product(WTE), refills(("scalar", lambda e, n: e.copy(n.R, n.ps))), *split_stages(lambda n: n.R[:, :, D:2 * D], nodeQ),
        ], T1, lambda n: n.R)
        sum_pass("mlp", T1)

        node_phase([
            ("vector", lambda e, n: e.tensor_scalar(n.st[1][:, 0:H].unsqueeze(2), n.at(deg), 1.0, None, ALU.max)),
            *mean_stages(WTN, 1, True), *norm_stages(), *turn_stages(), *gat_stages(WG[0]),
        ], T2, lambda n: n.R)
        softmax_pass("gat", T2, HEADS1)

        def plus_row(k):
            return ("vector", lambda e, n: e.tensor_tensor(n.Y, n.Y, bias_row(k), ALU.add))

        node_phase([
            *softmax_stages(HEADS1, ALU.add, SOFTMAX_EPS), plus_row(2),
            ("vector", lambda e, n: e.tensor_scalar(n.Y2, n.Y, 0.0, None, ALU.min)),
            ("scalar", lambda e, n: e.activation(n.Y2, n.Y2, ACT.Exp)),
            ("vector", lambda e, n: e.tensor_scalar(n.Y2, n.Y2, -1.0, None, ALU.add)),
            ("vector", lambda e, n: e.scalar_tensor_tensor(out=n.Y, in0=n.Y, scalar=0.0, in1=n.Y2,
                                                           op0=ALU.max, op1=ALU.add)),
            *turn_stages(), *gat_stages(WG[1]),
        ], T3, lambda n: n.R)
        softmax_pass("gat", T3, HEADS1)

        node_phase([
            *softmax_stages(HEADS1, ALU.add, SOFTMAX_EPS), plus_row(3),
            x_plus_y, clear_acc, ("vector", lambda e, n: e.tensor_copy(n.at(nodeM), const(2, HEADS1))),
            *norm_stages(), *turn_stages(),
            product(WX[:, 0:2 * D]), refills(plus_bias(lambda n: n.R, 4, 2)), product(WX[:, 2 * D:4 * D]),
            ("vector", lambda e, n: e.scalar_tensor_tensor(out=n.Y2, in0=n.ps[:, :, 0:D], scalar=Q_SCALE,
                                                           in1=bias_row(6), op0=ALU.mult, op1=ALU.add)),
            *split_stages(lambda n: n.Y2, nodeQ),
            plus_bias(lambda n: n.Y, 7, 1, D), x_plus_y,
        ], T4, lambda n: n.R)
        softmax_pass("dot", T4, HEADS3)

        node_phase([*softmax_stages(HEADS3, ALU.max, SOFTMAX_EPS), x_plus_y])
        chain([
            ("sync_dma", lambda e, i: e.dma_start(out[0:FULL * P, :].rearrange("(b p) f -> p b f", p=P), X[:, 0:FULL, :])),
            ("sync_dma", lambda e, i: e.dma_start(out[FULL * P:N, :], X[0:REST, FULL, :])),
        ])
        with nc.Block() as block:
            @block.sync
            def _(eng):
                table_ready(eng)


INPUTS = ["x", "src", "dst", "L0_gnn_W", "L0_gnn_b", "L1_gnn_W_edge", "L1_gnn_W_node", "L1_gnn_b_node",
          "L2_gnn_W1", "L2_gnn_a_src1", "L2_gnn_a_dst1", "L2_gnn_b1", "L2_gnn_W2", "L2_gnn_a_src2",
          "L2_gnn_a_dst2", "L2_gnn_b2", "L3_gnn_Wq", "L3_gnn_bq", "L3_gnn_Wk", "L3_gnn_bk", "L3_gnn_Wv",
          "L3_gnn_bv", "L3_gnn_Wskip", "L3_gnn_bskip"]


def kernel(**inputs):
    import numpy as np
    from concourse import bacc
    from concourse.bass_utils import run_bass_kernel_spmd

    nc = bacc.Bacc("TRN2", target_bir_lowering=False, num_devices=1)
    arrays, args = {}, []
    for name in INPUTS:
        a = np.ascontiguousarray(inputs[name])
        arrays[f"in_{name}"] = a
        args.append(nc.dram_tensor(f"in_{name}", a.shape, mybir.dt.from_np(a.dtype), kind="ExternalInput").ap())
    shape = inputs["x"].shape
    out = nc.dram_tensor("out", shape, F32, kind="ExternalOutput").ap()
    program(nc, *args, out)
    r = run_bass_kernel_spmd(nc, [arrays], core_ids=[0])
    return r.results[0]["out"]
```
